# Optimizing a Trainium2 kernel written in Bass

```python
import numpy as np
import jax
import jax.numpy as jnp

def _softmax(x, axis=-1):
    return jax.nn.softmax(x, axis=axis)

def _gelu(x):
    return jax.nn.gelu(x, approximate=True)

def _silu(x):
    return jax.nn.silu(x)

def _sigmoid(x):
    return jax.nn.sigmoid(x)

def _layernorm(x, axis=-1, eps=1e-05):
    m = jnp.mean(x, axis=axis, keepdims=True)
    v = jnp.var(x, axis=axis, keepdims=True)
    return (x - m) / jnp.sqrt(v + eps)

def _scatter_add(tgt, idx, src, axis=0):
    return tgt.at[idx].add(src)

def _segment_sum(src, seg, n):
    return jax.ops.segment_sum(src, seg, n)
kernel_name = 'mk_pixart_seq_d2_seqx_r8_95f3ec'

def setup_inputs(seed: int=0):
    np.random.seed(seed)
    _w = jnp.asarray

    def _rec_inputs():
        import jax
        import jax.numpy as jnp
        _rk = jax.random.key(seed)
        x = 7.22e-05 + 1 * jax.random.normal(jax.random.fold_in(_rk, 1), (1, 1024, 128), jnp.float32)
        _lenS = 1024 - jax.random.randint(jax.random.fold_in(_rk, 7), (1,), 0, max(1, 1024 // 4) + 1, jnp.int32)
        _lenS2 = 6404 - jax.random.randint(jax.random.fold_in(_rk, 8), (1,), 0, max(1, 6404 // 4) + 1, jnp.int32)
        cond_1024 = 0.0061147 + 1.02565 * jax.random.normal(jax.random.fold_in(_rk, 11), (1, 128), jnp.float32)
        _ctx_1024P = jax.random.normal(jax.random.fold_in(_rk, 12), (1, 16, 128), jnp.float32)
        _ctx_1024c = jax.random.dirichlet(jax.random.fold_in(_rk, 512), 0.3 * jnp.ones((16,), jnp.float32), (1, 6404))
        _ctx_1024t = jnp.einsum('bsk,bkd->bsd', _ctx_1024c, _ctx_1024P)
        _ctx_1024t = _ctx_1024t * jax.lax.rsqrt(jnp.mean(jnp.square(_ctx_1024t)) + 1e-12) * 0.953939
        ctx_1024 = 0.000376506 + 0.999991 * (_ctx_1024t + 0.3 * jax.random.normal(jax.random.fold_in(_rk, 612), (1, 6404, 128), jnp.float32))
        return (x, cond_1024, ctx_1024)
    x, cond_1024, ctx_1024 = _rec_inputs()

    def _L0_xcond_setup():
        import jax, jax.numpy as jnp
        import numpy as np
        EPS = 1e-06
        H = 16

        def layer_norm(x, gamma=None, beta=None):
            x32 = x.astype(jnp.float32)
            mu = jnp.mean(x32, axis=-1, keepdims=True)
            var = jnp.var(x32, axis=-1, keepdims=True)
            y = (x32 - mu) * jax.lax.rsqrt(var + EPS)
            if gamma is not None:
                y = y * gamma + beta
            return y.astype(x.dtype)

        def mha(q, k, v):
            B, Nq, C = q.shape
            d = C // H
            qh = q.reshape(B, Nq, H, d)
            kh = k.reshape(B, k.shape[1], H, d)
            vh = v.reshape(B, v.shape[1], H, d)
            scores = jnp.einsum('bqhd,bkhd->bhqk', qh, kh) / jnp.sqrt(jnp.asarray(d, q.dtype))
            attn = jax.nn.softmax(scores, axis=-1)
            out = jnp.einsum('bhqk,bkhd->bqhd', attn, vh)
            return out.reshape(B, Nq, C)
        key = jax.random.key(seed)
        ks = jax.random.split(key, 24)
        B, N, C, M, Cc = (4, 256, 128, 128, 128)
        hid = 4 * C
        s = 0.02
        return {'x': jax.random.normal(ks[0], (B, N, C), jnp.float32), 'mod': jax.random.normal(ks[1], (B, C), jnp.float32), 'context': jax.random.normal(ks[2], (B, M, Cc), jnp.float32), 'ada_w': jax.random.normal(ks[3], (C, 6 * C), jnp.float32) * s, 'ada_b': jnp.zeros((6 * C,), jnp.float32), 'qkv_w': jax.random.normal(ks[4], (C, 3 * C), jnp.float32) * s, 'qkv_b': jnp.zeros((3 * C,), jnp.float32), 'self_o_w': jax.random.normal(ks[5], (C, C), jnp.float32) * s, 'self_o_b': jnp.zeros((C,), jnp.float32), 'norm2_g': jnp.ones((C,), jnp.float32), 'norm2_b': jnp.zeros((C,), jnp.float32), 'q_w': jax.random.normal(ks[6], (C, C), jnp.float32) * s, 'q_b': jnp.zeros((C,), jnp.float32), 'kv_w': jax.random.normal(ks[7], (Cc, 2 * C), jnp.float32) * s, 'kv_b': jnp.zeros((2 * C,), jnp.float32), 'cross_o_w': jax.random.normal(ks[8], (C, C), jnp.float32) * s, 'cross_o_b': jnp.zeros((C,), jnp.float32), 'mlp_w1': jax.random.normal(ks[9], (C, hid), jnp.float32) * s, 'mlp_b1': jnp.zeros((hid,), jnp.float32), 'mlp_w2': jax.random.normal(ks[10], (hid, C), jnp.float32) * s, 'mlp_b2': jnp.zeros((C,), jnp.float32)}
    _L0_xcond_all = _L0_xcond_setup()
    _L0_xcond_in = {k: v for k, v in _L0_xcond_all.items() if k in ('ada_w', 'ada_b', 'qkv_w', 'qkv_b', 'self_o_w', 'self_o_b', 'norm2_g', 'norm2_b', 'q_w', 'q_b', 'kv_w', 'kv_b', 'cross_o_w', 'cross_o_b', 'mlp_w1', 'mlp_b1', 'mlp_w2', 'mlp_b2')}
    del _L0_xcond_all

    def _L1_xcond_setup():
        import jax, jax.numpy as jnp
        import numpy as np
        EPS = 1e-05

        def _ada_ln(x, c, W_ss, b_ss):
            mu = jnp.mean(x, axis=-1, keepdims=True)
            var = jnp.mean((x - mu) ** 2, axis=-1, keepdims=True)
            h = (x - mu) / jnp.sqrt(var + EPS)
            ss = jax.nn.silu(c) @ W_ss + b_ss
            scale, bias = jnp.split(ss, 2, axis=-1)
            return (1.0 + scale)[:, None, :] * h + bias[:, None, :]
        key = jax.random.key(seed)
        ks = jax.random.split(key, 12)
        B, Lq, Lkv, H = (8, 256, 64, 128)
        s = 0.02
        return {'x_q': jax.random.normal(ks[0], (B, Lq, H), jnp.float32), 'x_kv': jax.random.normal(ks[1], (B, Lkv, H), jnp.float32), 't_vec': jax.random.normal(ks[2], (B, H), jnp.float32), 'Wq': jax.random.normal(ks[3], (H, H), jnp.float32) * s, 'bq': jnp.zeros((H,), jnp.float32), 'Wkv': jax.random.normal(ks[4], (H, 2 * H), jnp.float32) * s, 'bkv': jnp.zeros((2 * H,), jnp.float32), 'Wp': jax.random.normal(ks[5], (H, H), jnp.float32) * s, 'bp': jnp.zeros((H,), jnp.float32), 'Wss_q': jax.random.normal(ks[6], (H, 2 * H), jnp.float32) * s, 'bss_q': jnp.zeros((2 * H,), jnp.float32), 'Wss_kv': jax.random.normal(ks[7], (H, 2 * H), jnp.float32) * s, 'bss_kv': jnp.zeros((2 * H,), jnp.float32)}
    _L1_xcond_all = _L1_xcond_setup()
    _L1_xcond_in = {k: v for k, v in _L1_xcond_all.items() if k in ('Wq', 'bq', 'Wkv', 'bkv', 'Wp', 'bp', 'Wss_q', 'bss_q', 'Wss_kv', 'bss_kv')}
    del _L1_xcond_all
    return {'x': x, 'cond_1024': cond_1024, 'ctx_1024': ctx_1024, 'L0_xcond_ada_w': _L0_xcond_in['ada_w'], 'L0_xcond_ada_b': _L0_xcond_in['ada_b'], 'L0_xcond_qkv_w': _L0_xcond_in['qkv_w'], 'L0_xcond_qkv_b': _L0_xcond_in['qkv_b'], 'L0_xcond_self_o_w': _L0_xcond_in['self_o_w'], 'L0_xcond_self_o_b': _L0_xcond_in['self_o_b'], 'L0_xcond_norm2_g': _L0_xcond_in['norm2_g'], 'L0_xcond_norm2_b': _L0_xcond_in['norm2_b'], 'L0_xcond_q_w': _L0_xcond_in['q_w'], 'L0_xcond_q_b': _L0_xcond_in['q_b'], 'L0_xcond_kv_w': _L0_xcond_in['kv_w'], 'L0_xcond_kv_b': _L0_xcond_in['kv_b'], 'L0_xcond_cross_o_w': _L0_xcond_in['cross_o_w'], 'L0_xcond_cross_o_b': _L0_xcond_in['cross_o_b'], 'L0_xcond_mlp_w1': _L0_xcond_in['mlp_w1'], 'L0_xcond_mlp_b1': _L0_xcond_in['mlp_b1'], 'L0_xcond_mlp_w2': _L0_xcond_in['mlp_w2'], 'L0_xcond_mlp_b2': _L0_xcond_in['mlp_b2'], 'L1_xcond_Wq': _L1_xcond_in['Wq'], 'L1_xcond_bq': _L1_xcond_in['bq'], 'L1_xcond_Wkv': _L1_xcond_in['Wkv'], 'L1_xcond_bkv': _L1_xcond_in['bkv'], 'L1_xcond_Wp': _L1_xcond_in['Wp'], 'L1_xcond_bp': _L1_xcond_in['bp'], 'L1_xcond_Wss_q': _L1_xcond_in['Wss_q'], 'L1_xcond_bss_q': _L1_xcond_in['bss_q'], 'L1_xcond_Wss_kv': _L1_xcond_in['Wss_kv'], 'L1_xcond_bss_kv': _L1_xcond_in['bss_kv']}

def reference(x, cond_1024, ctx_1024, L0_xcond_ada_w, L0_xcond_ada_b, L0_xcond_qkv_w, L0_xcond_qkv_b, L0_xcond_self_o_w, L0_xcond_self_o_b, L0_xcond_norm2_g, L0_xcond_norm2_b, L0_xcond_q_w, L0_xcond_q_b, L0_xcond_kv_w, L0_xcond_kv_b, L0_xcond_cross_o_w, L0_xcond_cross_o_b, L0_xcond_mlp_w1, L0_xcond_mlp_b1, L0_xcond_mlp_w2, L0_xcond_mlp_b2, L1_xcond_Wq, L1_xcond_bq, L1_xcond_Wkv, L1_xcond_bkv, L1_xcond_Wp, L1_xcond_bp, L1_xcond_Wss_q, L1_xcond_bss_q, L1_xcond_Wss_kv, L1_xcond_bss_kv):
    import jax
    import jax.numpy as jnp

    def _L0_xcond_ref(x, mod, context, ada_w, ada_b, qkv_w, qkv_b, self_o_w, self_o_b, norm2_g, norm2_b, q_w, q_b, kv_w, kv_b, cross_o_w, cross_o_b, mlp_w1, mlp_b1, mlp_w2, mlp_b2):
        import jax, jax.numpy as jnp
        import numpy as np
        EPS = 1e-06
        H = 16

        def layer_norm(x, gamma=None, beta=None):
            x32 = x.astype(jnp.float32)
            mu = jnp.mean(x32, axis=-1, keepdims=True)
            var = jnp.var(x32, axis=-1, keepdims=True)
            y = (x32 - mu) * jax.lax.rsqrt(var + EPS)
            if gamma is not None:
                y = y * gamma + beta
            return y.astype(x.dtype)

        def mha(q, k, v):
            B, Nq, C = q.shape
            d = C // H
            qh = q.reshape(B, Nq, H, d)
            kh = k.reshape(B, k.shape[1], H, d)
            vh = v.reshape(B, v.shape[1], H, d)
            scores = jnp.einsum('bqhd,bkhd->bhqk', qh, kh) / jnp.sqrt(jnp.asarray(d, q.dtype))
            attn = jax.nn.softmax(scores, axis=-1)
            out = jnp.einsum('bhqk,bkhd->bqhd', attn, vh)
            return out.reshape(B, Nq, C)
        C = x.shape[-1]
        m = jax.nn.silu(mod) @ ada_w + ada_b
        shift_msa, scale_msa, gate_msa, shift_mlp, scale_mlp, gate_mlp = [c[:, None, :] for c in jnp.split(m, 6, axis=-1)]
        h = layer_norm(x)
        h = h * (1.0 + scale_msa) + shift_msa
        qkv = h @ qkv_w + qkv_b
        q, k, v = jnp.split(qkv, 3, axis=-1)
        h = mha(q, k, v) @ self_o_w + self_o_b
        x = x + h * gate_msa
        h = layer_norm(x, norm2_g, norm2_b)
        q = h @ q_w + q_b
        kv = context @ kv_w + kv_b
        k, v = jnp.split(kv, 2, axis=-1)
        h = mha(q, k, v) @ cross_o_w + cross_o_b
        x = x + h
        h = layer_norm(x)
        h = h * (1.0 + scale_mlp) + shift_mlp
        h = jax.nn.gelu(h @ mlp_w1 + mlp_b1) @ mlp_w2 + mlp_b2
        x = x + h * gate_mlp
        return x

    def _L1_xcond_ref(x_q, x_kv, t_vec, Wq, bq, Wkv, bkv, Wp, bp, Wss_q, bss_q, Wss_kv, bss_kv):
        import jax, jax.numpy as jnp
        import numpy as np
        EPS = 1e-05

        def _ada_ln(x, c, W_ss, b_ss):
            mu = jnp.mean(x, axis=-1, keepdims=True)
            var = jnp.mean((x - mu) ** 2, axis=-1, keepdims=True)
            h = (x - mu) / jnp.sqrt(var + EPS)
            ss = jax.nn.silu(c) @ W_ss + b_ss
            scale, bias = jnp.split(ss, 2, axis=-1)
            return (1.0 + scale)[:, None, :] * h + bias[:, None, :]
        B, Lq, H = x_q.shape
        Lkv = x_kv.shape[1]
        nh = 16
        dh = H // nh
        xq = _ada_ln(x_q, t_vec, Wss_q, bss_q)
        xkv = _ada_ln(x_kv, t_vec, Wss_kv, bss_kv)
        q = (xq @ Wq + bq).reshape(B, Lq, nh, dh)
        kv = (xkv @ Wkv + bkv).reshape(B, Lkv, 2, nh, dh)
        k = kv[:, :, 0]
        v = kv[:, :, 1]
        scores = jnp.einsum('bqhd,bkhd->bhqk', q, k) / jnp.sqrt(jnp.float32(dh))
        attn = jax.nn.softmax(scores, axis=-1)
        out = jnp.einsum('bhqk,bkhd->bqhd', attn, v).reshape(B, Lq, H)
        return x_q + (out @ Wp + bp)
    x = _L0_xcond_ref(x, cond_1024, ctx_1024, L0_xcond_ada_w, L0_xcond_ada_b, L0_xcond_qkv_w, L0_xcond_qkv_b, L0_xcond_self_o_w, L0_xcond_self_o_b, L0_xcond_norm2_g, L0_xcond_norm2_b, L0_xcond_q_w, L0_xcond_q_b, L0_xcond_kv_w, L0_xcond_kv_b, L0_xcond_cross_o_w, L0_xcond_cross_o_b, L0_xcond_mlp_w1, L0_xcond_mlp_b1, L0_xcond_mlp_w2, L0_xcond_mlp_b2)
    x = _L1_xcond_ref(x, ctx_1024, cond_1024, L1_xcond_Wq, L1_xcond_bq, L1_xcond_Wkv, L1_xcond_bkv, L1_xcond_Wp, L1_xcond_bp, L1_xcond_Wss_q, L1_xcond_bss_q, L1_xcond_Wss_kv, L1_xcond_bss_kv)
    return x

_drawn_inputs = setup_inputs


def setup_inputs(seed=0):
    import zlib

    import numpy as np

    out = dict(_drawn_inputs(seed))
    spreads = {'L0_xcond_ada_b': (0.0, 0.467),
     'L0_xcond_qkv_b': (0.0, 0.8),
     'L0_xcond_self_o_b': (0.0, 0.428),
     'L0_xcond_norm2_g': (1.0, 0.6),
     'L0_xcond_norm2_b': (0.0, 2.0),
     'L0_xcond_q_b': (0.0, 2.0),
     'L0_xcond_kv_b': (0.0, 0.361),
     'L0_xcond_cross_o_b': (0.0, 0.1),
     'L0_xcond_mlp_b1': (0.0, 0.8),
     'L0_xcond_mlp_b2': (0.0, 0.478),
     'L1_xcond_bq': (0.0, 2.0),
     'L1_xcond_bkv': (0.0, 0.335),
     'L1_xcond_bp': (0.0, 0.1),
     'L1_xcond_bss_q': (0.0, 2.0),
     'L1_xcond_bss_kv': (0.0, 2.0)}
    factors = {'L0_xcond_qkv_w': 8.0,
     'L0_xcond_self_o_w': 8.0,
     'L0_xcond_q_w': 8.0,
     'L0_xcond_kv_w': 2.737,
     'L0_xcond_mlp_w1': 5.872,
     'L0_xcond_mlp_w2': 5.136,
     'L1_xcond_Wq': 39.937,
     'L1_xcond_Wss_q': 49.002,
     'L1_xcond_Wss_kv': 8.0}
    for name, (base, spread) in spreads.items():
        noise = np.random.default_rng([zlib.crc32(name.encode()), seed]).standard_normal(out[name].shape)
        drawn = base * np.exp(spread * noise) if base else spread * noise
        out[name] = jnp.asarray(drawn.astype(out[name].dtype))
    for name, factor in factors.items():
        out[name] = (out[name] * factor).astype(out[name].dtype)
    return out
```

```python
from contextlib import ExitStack

import concourse.bass as bass
from concourse import mybir

ALU = mybir.AluOpType
ACT = mybir.ActivationFunctionType
AX_X = mybir.AxisListType.X
F32 = mybir.dt.float32
BF16 = mybir.dt.bfloat16

P = 128
HEADS = 16
DH = P // HEADS
QN = 1024
QT = QN // P
HALF = 512
CTX = 6404
SCALE = float(DH) ** -0.5
PARTS = 3
BLOCK = 32
MROW = PARTS * BLOCK
KROWS = MROW + PARTS
VW = 32
MCH = 1024
LOOKAHEAD = 3


def ceil_div(a, b):
    return -(-a // b)


def batches(units):
    return [list(range(u, min(u + 4, units))) for u in range(0, units, 4)]


class Attention:

    def __init__(self, name, keys):
        self.name, self.keys = name, keys
        self.kt = ceil_div(keys, P)
        self.units = 2 * self.kt
        self.batches = batches(self.units)
        self.nb = len(self.batches)
        self.max_chunks = [(t, c, min(MCH, keys - c)) for t in range(QT) for c in range(0, keys, MCH)]
        self.per_tile = ceil_div(keys, MCH)
        self.nm = len(self.max_chunks) + 1
        last = self.nb - 3
        self.chunks_at = [[] for _ in range(self.nb)]
        for c in range(self.nm - 1):
            self.chunks_at[c * last // (self.nm - 1)].append(c)
        self.turn_at = last
        self.pieces = [(0, self.kt)] if self.kt < 16 else [(a, min(a + 13, self.kt)) for a in range(0, self.kt, 13)]
        self.loads = PARTS * PARTS * (len(self.pieces) + 1)
        assert self.nb % 2 == 0 and self.units % 2 == 0 and self.nb > LOOKAHEAD


class Chunk:

    def __init__(self, source, first, rows, eps, scale, shift, projections=(), values=None, mlp=False):
        self.source, self.first, self.rows, self.eps = source, first, rows, eps
        self.scale, self.shift = scale, shift
        self.projections, self.values, self.mlp = projections, values, mlp
        self.tiles = [min(P, rows - a) for a in range(0, rows, P)]


BIAS_ROWS = ["L0_xcond_ada_b", "L0_xcond_qkv_b", "L0_xcond_norm2_g", "L0_xcond_norm2_b", "L0_xcond_q_b",
             "L0_xcond_kv_b", "L0_xcond_mlp_b1", "L1_xcond_bq", "L1_xcond_bkv", "L1_xcond_bss_q",
             "L1_xcond_bss_kv", "cond_1024"]


def pixart_program(nc, a, out):
    col, n = {}, 0
    for name in BIAS_ROWS:
        size = 1
        for s in a[name].shape:
            size *= s
        col[name] = n
        n += size // P
    NCOL = n

    attentions = {n: Attention(n, k) for n, k in (("own", QN), ("cross", CTX), ("last", CTX))}

    dram = {}
    for n, at in attentions.items():
        dram[n, "q"] = nc.dram_tensor(f"{n}_q_parts", (PARTS, P, QN), BF16, kind="Internal").ap()
        dram[n, "k"] = nc.dram_tensor(f"{n}_k_parts", (PARTS, P, at.keys), BF16, kind="Internal").ap()
        dram[n, "o"] = nc.dram_tensor(f"{n}_heads_out", (2, 2, P, QN), F32, kind="Internal").ap()

    with ExitStack() as ctx:
        def sb(name, shape, dt=F32):
            return ctx.enter_context(nc.sbuf_tensor(name, shape, dt))

        sems = {}

        def sem(name):
            if name not in sems:
                sems[name] = ctx.enter_context(nc.semaphore(name))
            return sems[name]

        ps = ctx.enter_context(nc.psum_tensor("ps", [P, 8, HALF], F32))
        S_BANK, O_BANK, M_BANK = 0, 2, 4
        T_BANK, J_BANK, V_BANK = 0, 2, 4

        KTILES = attentions["cross"].kt
        kh = [sb(f"kh{i}", [P, KTILES * P], BF16) for i in range(2)]
        qh = [sb(f"qh{i}", [P, QN], BF16) for i in range(2)]
        v_all = sb("v_all", [P, KTILES, P])
        vh = [sb(f"vh{i}", [P, KTILES, VW]) for i in range(2)]
        probs = sb("probs", [P, 2, 4, HALF])
        heads_out = [sb(f"heads_out{i}", [P, HALF]) for i in range(2)]
        max_part = sb("max_part", [P, QT, ceil_div(CTX, MCH)])
        neg_max = sb("neg_max", [P, QT])
        max_rest = sb("max_rest", [P, QT])
        max_parts = sb("max_parts", [P, PARTS, QT], BF16)
        max_rows = [sb(f"max_rows{i}", [PARTS * QT, P], BF16) for i in range(2)]
        nd = sb("nd", [P, 2, 2, QN])
        x = sb("x", [P, QT, P])
        nat = sb("nat", [P, 2, 4, P])
        xh = sb("xh", [P, 2, 4, P])
        h_t = sb("h_t", [P, 2, HALF])
        kf = sb("kf", [P, 2, HALF])
        kr = sb("kr", [P, 2, HALF])
        kp = sb("kp", [P, 2, PARTS, HALF], BF16)
        hid = sb("hid", [P, 4, HALF])
        tmp = sb("tmp", [P, 2, 4, P])
        stats = sb("stats", [P, 4, 6])
        mv = sb("mv", [P, 4, 2])
        sd = sb("sd", [P, 4])
        rstd = sb("rstd", [P, 4])
        ident = sb("ident", [P, P])
        ident16 = sb("ident16", [P, P], BF16)
        rows = sb("rows", [P, P])
        cols = sb("cols", [P, NCOL])
        one_cols = sb("one_cols", [P, 2])
        credits = sb("credits", [P, 16])
        silu = sb("silu", [P, 4])
        silu_wide = sb("silu_wide", [P, P])
        shifts = sb("shifts", [P, 8])
        scales = sb("scales", [P, 8])
        gates = sb("gates", [P, 2, P])
        wide = {n: sb(f"wide_{n}", [P, P]) for n in ("gate0", "gate1", "self_o", "cross_o", "mlp", "last")}

        w = {}
        for n, width in (("L0_xcond_ada_w", 6), ("L0_xcond_qkv_w", 3), ("L0_xcond_self_o_w", 1), ("L0_xcond_q_w", 1),
                         ("L0_xcond_kv_w", 2), ("L0_xcond_cross_o_w", 1), ("L0_xcond_mlp_w1", 4),
                         ("L0_xcond_mlp_w2", 4), ("L1_xcond_Wq", 1), ("L1_xcond_Wkv", 2), ("L1_xcond_Wp", 1),
                         ("L1_xcond_Wss_q", 2), ("L1_xcond_Wss_kv", 2)):
            w[n] = sb("w_" + n, [P, width, P])

        x_dram = a["x"].rearrange("o (t p) c -> p (o t) c", p=P)
        out_dram = out.rearrange("o (t p) c -> p (o t) c", p=P)
        ctx_dram = a["ctx_1024"].rearrange("o n c -> (o n) c")

        MSA, MLP, SSQ, SSKV = 0, 1, 2, 3
        ab, bq, bk = col["L0_xcond_ada_b"], col["L1_xcond_bss_q"], col["L1_xcond_bss_kv"]
        MODS = [("L0_xcond_ada_w", 0, 1, ab + 0, ab + 1), ("L0_xcond_ada_w", 3, 4, ab + 3, ab + 4),
                ("L1_xcond_Wss_q", 1, 0, bq + 1, bq + 0), ("L1_xcond_Wss_kv", 1, 0, bk + 1, bk + 0)]
        GATES = [2, 5]

        def mod(k):
            return scales[:, k:k + 1], shifts[:, k:k + 1]

        norm2 = (cols[:, col["L0_xcond_norm2_g"]:col["L0_xcond_norm2_g"] + 1],
                 cols[:, col["L0_xcond_norm2_b"]:col["L0_xcond_norm2_b"] + 1])
        plain = (one_cols[:, 0:1], one_cols[:, 1:2])

        def proj(weights, k, bias, k2, dst, first):
            c = col[bias] + k2
            return (w[weights][:, k, :], cols[:, c:c + 1], dst, first)

        def token_chunks(make):
            return [make(f) for f in range(0, QN, HALF)]

        def ctx_chunks(make):
            return [make(f, min(HALF, CTX - f)) for f in range(0, CTX, HALF)]

        GROUPS = {
            "own": token_chunks(lambda f: Chunk(
                "x", f, HALF, 1e-6, *mod(MSA),
                [proj("L0_xcond_qkv_w", 0, "L0_xcond_qkv_b", 0, dram["own", "q"], f),
                 proj("L0_xcond_qkv_w", 1, "L0_xcond_qkv_b", 1, dram["own", "k"], f)],
                w["L0_xcond_qkv_w"][:, 2, :])),
            "cross": ctx_chunks(lambda f, r: Chunk(
                "ctx", f, r, None, *plain,
                [proj("L0_xcond_kv_w", 0, "L0_xcond_kv_b", 0, dram["cross", "k"], f)],
                w["L0_xcond_kv_w"][:, 1, :]))
            + token_chunks(lambda f: Chunk(
                "x", f, HALF, 1e-6, *norm2,
                [proj("L0_xcond_q_w", 0, "L0_xcond_q_b", 0, dram["cross", "q"], f)])),
            "mlp": token_chunks(lambda f: Chunk("x", f, HALF, 1e-6, *mod(MLP), mlp=True)),
            "last": ctx_chunks(lambda f, r: Chunk(
                "ctx", f, r, 1e-5, *mod(SSKV),
                [proj("L1_xcond_Wkv", 0, "L1_xcond_bkv", 0, dram["last", "k"], f)],
                w["L1_xcond_Wkv"][:, 1, :]))
            + token_chunks(lambda f: Chunk(
                "x", f, HALF, 1e-5, *mod(SSQ),
                [proj("L1_xcond_Wq", 0, "L1_xcond_bq", 0, dram["last", "q"], f)])),
        }
        ORDER = ["own", "cross", "mlp", "last"]

        all_chunks = [c for g in ORDER for c in GROUPS[g]]
        loads, ln, pj, vj, mo = 0, 0, 0, 0, 0
        for i, c in enumerate(all_chunks):
            c.i = i
            c.load = loads
            loads += c.source == "ctx"
            c.norm = ln
            ln += c.eps is not None
            c.norm_upto = ln
            c.pj = pj
            pj += len(c.projections) + (4 if c.mlp else 0)
            c.pj_upto = pj
            c.vj = vj
            vj += c.values is not None or c.mlp
            c.vj_upto = vj
        stored = {}
        n_store = [0, 0]
        for c in all_chunks:
            if not c.mlp:
                for k in range(c.pj, c.pj_upto):
                    stored[k] = n_store[k % 2]
                    n_store[k % 2] += 1
        stores_upto = {}
        run = [0, 0]
        for g in ORDER:
            for c in GROUPS[g]:
                if not c.mlp:
                    for k in range(c.pj, c.pj_upto):
                        run[k % 2] += 1
            stores_upto[g] = tuple(run)

        k_ready, n = {}, 0
        for c in all_chunks:
            if not c.mlp:
                for k in range(c.pj, c.pj_upto):
                    n += 1
                    k_ready[k] = n
        ctx_ready, n = {}, [0, 0]
        for c in all_chunks:
            if c.source == "ctx":
                n[c.load % 2] += 16 * (1 + (c.rows % P > 0))
                ctx_ready[c.i] = n[c.load % 2]
        ATT = list(attentions)

        def pipeline(group, normalise, turn, project):
            g = GROUPS[group]
            for s in range(-2, len(g)):
                if normalise and s + 2 < len(g):
                    normalise(g[s + 2])
                if turn and 0 <= s + 1 < len(g):
                    turn(g[s + 1])
                if project and s >= 0:
                    project(g[s])

        def chunk_source(c, t):
            if c.source == "x":
                return x[0:c.tiles[t], c.first // P + t, :]
            return nat[0:c.tiles[t], c.load % 2, t, :]

        def head_pairs(eng, slot):
            with eng.Fori(0, HEADS // 2 - 1) as i:
                slot(2 * i, 0, True, True)
                slot(2 * i + 1, 1, True, True)
            slot(HEADS - 2, 0, True, False)
            slot(HEADS - 1, 1, False, False)

        block = ctx.enter_context(nc.Block())

        @block.sync
        def _(sp):
            for name in BIAS_ROWS:
                v = a[name]
                v = v.rearrange("o (r p) -> (o r) p", p=P) if len(v.shape) == 2 else v.rearrange("(r p) -> r p", p=P)
                sp.dma_start(rows[col[name]:col[name] + v.shape[0], :], v).then_inc(sem("rows_loaded"), 16)
            sp.dma_start(x[:, :, :], x_dram).then_inc(sem("x_loaded"), 16)
            for name, t in w.items():
                src = a[name].rearrange("(t p) n -> p t n", p=P) if name == "L0_xcond_mlp_w2" else \
                    a[name].rearrange("p (t n) -> p t n", n=P)
                sp.dma_start(t[:, :, :], src).then_inc(sem("weights_loaded"), 16)
            for n, v in (("gate0", a["L0_xcond_ada_b"][2 * P:3 * P]), ("gate1", a["L0_xcond_ada_b"][5 * P:6 * P]),
                         ("self_o", a["L0_xcond_self_o_b"]), ("cross_o", a["L0_xcond_cross_o_b"]),
                         ("mlp", a["L0_xcond_mlp_b2"]), ("last", a["L1_xcond_bp"])):
                sp.dma_start(wide[n][:, :], v.partition_broadcast(P)).then_inc(sem("wide_loaded"), 16)

            def load_ctx(c):
                if c.source != "ctx":
                    return
                if c.load >= 2:
                    prev = next(d for d in all_chunks if d.source == "ctx" and d.load == c.load - 2)
                    sp.wait_ge(sem("turned"), prev.i + 1)
                s = sem(f"ctx_loaded{c.load % 2}")
                full = c.rows // P
                sp.dma_start(nat[:, c.load % 2, 0:full, :],
                             ctx_dram[c.first:c.first + full * P, :].rearrange("(t p) n -> p t n", p=P)).then_inc(s, 16)
                if c.rows % P:
                    sp.dma_start(nat[0:c.rows % P, c.load % 2, full, :],
                                 ctx_dram[c.first + full * P:c.first + c.rows, :]).then_inc(s, 16)

            def store_parts(c):
                if c.mlp:
                    return
                for k, (_, _, dst, first) in zip(range(c.pj, c.pj_upto), c.projections):
                    sp.wait_ge(sem("parts_ready"), k_ready[k])
                    sp.dma_start(dst[:, :, first:first + c.rows].rearrange("j f n -> f j n"),
                                 kp[:, k % 2, :, 0:c.rows]).then_inc(sem(f"parts_stored{k % 2}"), 16)

            def attention(at):
                S = lambda n: sem(f"{at.name}_{n}")
                q_parts, k_parts, o_dram = (dram[at.name, n] for n in "qko")

                def load_keys(h, p, piece):
                    c0, c1 = piece[0] * P, min(piece[1] * P, at.keys)
                    for j in range(PARTS):
                        for r in range(PARTS):
                            sp.dma_start(kh[p][BLOCK * j + DH * r:BLOCK * j + DH * (r + 1), c0:c1],
                                         k_parts[j, bass.ds(h * DH, DH), c0:c1]).then_inc(S(f"operands{p}"), 16)

                def load_queries(h, p):
                    for j in range(PARTS):
                        for r in range(PARTS):
                            sp.dma_start(qh[p][BLOCK * j + DH * r:BLOCK * j + DH * (r + 1), :],
                                         q_parts[r, bass.ds(h * DH, DH), :]).then_inc(S(f"operands{p}"), 16)

                def store_max(h, p, heads_before):
                    sp.wait_ge(S("heads_stored"), 8 * 16 * heads_before + 16)
                    sp.wait_ge(S("max_free"), at.nm * (h + 1) + 2)
                    for j in range(PARTS):
                        sp.dma_start(qh[p][MROW + j:MROW + j + 1, :].rearrange("o (t q) -> o t q", q=P),
                                     max_rows[p][QT * j:QT * (j + 1), :]).then_inc(S(f"max_loaded{p}"), 16)

                for k, n in enumerate(stores_upto[at.name]):
                    sp.wait_ge(sem(f"parts_stored{k}"), 16 * n)
                sp.wait_ge(sem("zeroed"), 1)
                for h in range(2):
                    load_queries(h, h)
                    for piece in at.pieces:
                        load_keys(h, h, piece)
                store_max(0, 0, 0)

                def slot(h, p, has_next, has_next2):
                    if has_next2:
                        for piece in at.pieces[:-1]:
                            sp.wait_ge(S("scored"), at.units * h + 2 * piece[1])
                            load_keys(h + 2, p, piece)
                    if has_next:
                        store_max(h + 1, 1 - p, h)
                    if has_next2:
                        sp.wait_ge(S("scored"), at.units * (h + 1))
                        load_queries(h + 2, p)
                        load_keys(h + 2, p, at.pieces[-1])
                    sp.wait_ge(S("closed"), h + 1 + 2)
                    for g in range(4):
                        for n in range(2):
                            rows_of = slice(BLOCK * g + DH * n, BLOCK * g + DH * (n + 1))
                            sp.dma_start(o_dram[g // 2, n, bass.ds(h * DH, DH), (g % 2) * HALF:(g % 2 + 1) * HALF],
                                         heads_out[p][rows_of, :]).then_inc(S("heads_stored"), 16)
                head_pairs(sp, slot)
                sp.wait_ge(S("heads_stored"), 8 * 16 * HEADS + 16)
                for g in range(2):
                    for n in range(2):
                        sp.dma_start(nd[:, g, n, :], o_dram[g, n, :, :]).then_inc(S("sums_loaded"), 16)

            pipeline("own", load_ctx, None, store_parts)
            attention(attentions["own"])
            pipeline("cross", load_ctx, None, store_parts)
            attention(attentions["cross"])
            pipeline("last", load_ctx, None, store_parts)
            attention(attentions["last"])
            for t in range(2):
                sp.wait_ge(sem("tokens_done"), 2 * len(ATT) - 1 + t)
                sp.dma_start(out_dram[:, 4 * t:4 * t + 4, :], tmp[:, t, :, :]).then_inc(sem("out_stored"), 16)
            sp.wait_ge(sem("out_stored"), 32)

        @block.gpsimd
        def _(pool):
            nc.gpsimd.memset(ident[:, :], 0.0).then_inc(sem("pool"), 1)
            nc.gpsimd.memset(ident16[:, :], 0.0).then_inc(sem("pool"), 1)
            pool.wait_ge(sem("pool"), 2)
            for t in (ident, ident16):
                nc.gpsimd.affine_select(out=t[:, :], in_=t[:, :], compare_op=ALU.not_equal, fill=1.0, base=0,
                                        pattern=[[-1, P]], channel_multiplier=1).then_inc(sem("identities"), 1)
            nc.gpsimd.memset(v_all[:, KTILES - 1, :], 0.0).then_inc(sem("pool"), 1)
            for i in range(2):
                nc.gpsimd.memset(vh[i][:, :, :], 0.0).then_inc(sem("pool"), 1)
            pool.wait_ge(sem("pool"), 5)
            for i in range(2):
                nc.gpsimd.memset(vh[i][:, 0:KTILES - 1, DH:2 * DH], 1.0).then_inc(sem("pool"), 1)
                nc.gpsimd.memset(vh[i][0:CTX % P, KTILES - 1, DH:2 * DH], 1.0).then_inc(sem("pool"), 1)
            pool.wait_ge(sem("pool"), 9)

            def attention(at, vj):
                S = lambda n: sem(f"{at.name}_{n}")

                def copy_values(h, p):
                    nc.gpsimd.tensor_copy(vh[p][:, 0:at.kt, 0:DH], v_all[:, 0:at.kt, bass.ds(h * DH, DH)]
                                          ).then_inc(S("values"), 1)
                pool.wait_ge(sem("values_out"), vj)
                copy_values(0, 0)
                copy_values(1, 1)

                def slot(h, p, has_next, has_next2):
                    if has_next2:
                        pool.wait_ge(S("summed"), at.nb * (h + 1) + 2)
                        copy_values(h + 2, p)
                head_pairs(pool, slot)

            attention(attentions["own"], GROUPS["own"][-1].vj_upto)
            attention(attentions["cross"], GROUPS["cross"][-1].vj_upto)
            attention(attentions["last"], GROUPS["last"][-1].vj_upto)

        @block.scalar
        def _(act):
            act.wait_ge(sem("cols_ready"), 1)
            cc = col["cond_1024"]
            nc.scalar.activation(silu[:, 0:1], cols[:, cc:cc + 1], ACT.Exp, scale=-1.0).then_inc(sem("cond_exp"), 1)

            def root(c):
                if c.eps is None:
                    return
                act.wait_ge(sem("variances"), c.norm_upto)
                r = c.tiles[0]
                nc.scalar.activation(sd[0:r, 0:len(c.tiles)], sd[0:r, 0:len(c.tiles)], ACT.Sqrt).then_inc(sem("roots"), 1)

            def evacuate_turned(c):
                act.wait_ge(sem("turned"), c.i + 1)
                if c.i == 0:
                    act.wait_ge(sem("mods_ready"), 3)
                if c.i >= 2:
                    old = all_chunks[c.i - 2]
                    if old.values is not None:
                        act.wait_ge(sem("valued"), old.vj_upto)
                    else:
                        act.wait_ge(sem("projected"), old.pj_upto)
                nc.scalar.activation(h_t[:, c.i % 2, 0:c.rows], ps[:, T_BANK + c.i % 2, 0:c.rows], ACT.Identity,
                                     bias=c.shift, scale=c.scale).then_inc(sem("h_t_ready"), 1)

            def evacuate_projected(c):
                if c.mlp:
                    for f in range(4):
                        act.wait_ge(sem("projected"), c.pj + f + 1)
                        if f == 0 and c.vj > GROUPS["mlp"][0].vj:
                            act.wait_ge(sem("valued"), c.vj)
                        b1 = col["L0_xcond_mlp_b1"] + f
                        nc.scalar.activation(hid[:, f, :], ps[:, J_BANK + (c.pj + f) % 2, :], ACT.Gelu_apprx_tanh,
                                             bias=cols[:, b1:b1 + 1]).then_inc(sem("projected_free"), 1)
                    return
                for k, (_, bias, _, _) in zip(range(c.pj, c.pj_upto), c.projections):
                    act.wait_ge(sem("projected"), k + 1)
                    if stored[k]:
                        act.wait_ge(sem(f"parts_stored{k % 2}"), 16 * stored[k])
                    src = ps[:, J_BANK + k % 2, 0:c.rows]
                    nc.scalar.activation(kf[:, k % 2, 0:c.rows], src, ACT.Identity, bias=bias).then_inc(sem("kf_ready"), 1)
                    nc.scalar.activation(kp[:, k % 2, 0, 0:c.rows], src, ACT.Identity, bias=bias).then_inc(sem("projected_free"), 1)

            def attention(at):
                S = lambda n: sem(f"{at.name}_{n}")

                def exps(h, b):
                    act.wait_ge(S("summed"), at.nb * h + b + 1)
                    for n, u in enumerate(at.batches[b]):
                        act.wait_ge(S("scored"), at.units * h + u + 1)
                        nc.scalar.activation(probs[:, b % 2, n, :], ps[:, S_BANK + u % 2, :], ACT.Exp,
                                             scale=SCALE).then_inc(S("exps"), 1)

                def close(h, p):
                    act.wait_ge(S("summed"), at.nb * (h + 1) + 2)
                    nc.scalar.activation(heads_out[p][:, :], ps[:, O_BANK + p, :], ACT.Copy).then_inc(S("closed"), 1)

                for b in range(LOOKAHEAD):
                    exps(0, b)

                def slot(h, p, has_next, has_next2):
                    for b in range(LOOKAHEAD, at.nb):
                        exps(h, b)
                    if has_next:
                        for b in range(LOOKAHEAD):
                            exps(h + 1, b)
                    close(h, p)
                head_pairs(act, slot)

            pipeline("own", root, evacuate_turned, evacuate_projected)
            attention(attentions["own"])
            pipeline("cross", root, evacuate_turned, evacuate_projected)
            attention(attentions["cross"])
            pipeline("mlp", root, evacuate_turned, evacuate_projected)
            pipeline("last", root, evacuate_turned, evacuate_projected)
            attention(attentions["last"])

        @block.vector
        def _(dve):
            chain = [0]

            def link(ins):
                chain[0] += 1
                ins.then_inc(sem("dve_chain"), 1)
                dve.wait_ge(sem("dve_chain"), chain[0])

            for i in range(2):
                link(nc.vector.memset(kh[i][:, :], 0.0))
                link(nc.vector.memset(kh[i][MROW:KROWS, 0:CTX], 1.0))
                link(nc.vector.memset(qh[i][:, :], 0.0))
            link(nc.vector.memset(one_cols[:, 0:1], 1.0))
            nc.vector.memset(one_cols[:, 1:2], 0.0).then_inc(sem("zeroed"), 1)
            credit = iter(range(16))
            for at in attentions.values():
                for n, places in (("exps", 2), ("max_free", 2), ("summed", 2), ("closed", 2), ("heads_stored", 16)):
                    k = next(credit)
                    nc.vector.memset(credits[:, k:k + 1], 0.0).then_inc(sem(f"{at.name}_{n}"), places)

            dve.wait_ge(sem("cols_turned"), 1)
            nc.vector.tensor_copy(cols[:, :], ps[:, 0, 0:NCOL]).then_inc(sem("cols_ready"), 1)
            dve.wait_ge(sem("cols_ready"), 1)
            dve.wait_ge(sem("cond_exp"), 1)
            cc = col["cond_1024"]
            link(nc.vector.tensor_scalar_add(silu[:, 1:2], silu[:, 0:1], 1.0))
            link(nc.vector.reciprocal(silu[:, 2:3], silu[:, 1:2]))
            link(nc.vector.tensor_tensor(silu[:, 3:4], silu[:, 2:3], cols[:, cc:cc + 1], ALU.mult))
            nc.vector.tensor_copy(silu_wide[:, :], silu[:, 3:4].broadcast_to([P, P])).then_inc(sem("silu_ready"), 1)
            dve.wait_ge(sem("mods_product"), 1)
            for k, (_, _, _, cb, cs) in enumerate(MODS):
                link(nc.vector.tensor_tensor(shifts[:, k:k + 1], ps[:, 1, k:k + 1], cols[:, cb:cb + 1], ALU.add))
                link(nc.vector.tensor_tensor(scales[:, 4 + k:5 + k], ps[:, 1, 4 + k:5 + k], cols[:, cs:cs + 1], ALU.add))
            nc.vector.tensor_scalar_add(scales[:, 0:4], scales[:, 4:8], 1.0).then_inc(sem("mods_ready"), 1)
            dve.wait_ge(sem("wide_loaded"), 16 * len(wide))
            for k in range(2):
                nc.vector.tensor_tensor(gates[:, k, :], ps[:, 2, k * P:(k + 1) * P], wide[f"gate{k}"][:, :],
                                        ALU.add).then_inc(sem("mods_ready"), 1)

            def normalise(c):
                if c.eps is None:
                    return
                if c.source == "ctx":
                    dve.wait_ge(sem(f"ctx_loaded{c.load % 2}"), ctx_ready[c.i])
                elif c.i == 0:
                    dve.wait_ge(sem("x_loaded"), 16)
                if c.i >= 2:
                    dve.wait_ge(sem("turned"), c.i - 1)
                for t, r in enumerate(c.tiles):
                    last = nc.vector.bn_stats(stats[0:r, t, :], chunk_source(c, t))
                    last.then_inc(sem("dve_chain"), 1)
                    chain[0] += 1
                dve.wait_ge(sem("dve_chain"), chain[0])
                for t, r in enumerate(c.tiles):
                    nc.vector.bn_aggr(mv[0:r, t, :], stats[0:r, t, :]).then_inc(sem("dve_chain"), 1)
                    chain[0] += 1
                dve.wait_ge(sem("dve_chain"), chain[0])
                n_full = sum(r == P for r in c.tiles)
                if c.tiles[-1] != P:
                    link(nc.vector.memset(sd[:, n_full:n_full + 1], 1.0))
                    link(nc.vector.tensor_scalar_add(sd[0:c.tiles[-1], n_full:n_full + 1],
                                                     mv[0:c.tiles[-1], n_full, 1:2], c.eps))
                nc.vector.tensor_scalar_add(sd[:, 0:n_full], mv[:, 0:n_full, 1], c.eps).then_inc(sem("variances"), 1)
                dve.wait_ge(sem("roots"), c.norm_upto)
                link(nc.vector.reciprocal(rstd[:, 0:len(c.tiles)], sd[:, 0:len(c.tiles)]))
                for t, r in enumerate(c.tiles):
                    last = nc.vector.tensor_scalar(xh[0:r, c.i % 2, t, :], chunk_source(c, t), mv[0:r, t, 0:1],
                                                   rstd[0:r, t:t + 1], ALU.subtract, ALU.mult)
                last.then_inc(sem("normalised"), 1)

            def project(c):
                if c.mlp:
                    half = c.first // HALF
                    dve.wait_ge(sem("valued"), c.vj + 1)
                    product_out(V_BANK + c.vj % 2, half, "mlp", 1, "values_out", c.vj + 1)
                    return
                for k in range(c.pj, c.pj_upto):
                    dve.wait_ge(sem("kf_ready"), k_ready[k])
                    dve.wait_ge(sem("projected_free"), k + 1)
                    r = slice(0, c.rows)
                    link(nc.vector.tensor_tensor(kr[:, k % 2, r], kf[:, k % 2, r], kp[:, k % 2, 0, r], ALU.subtract))
                    link(nc.vector.tensor_copy(kp[:, k % 2, 1, r], kr[:, k % 2, r]))
                    nc.vector.tensor_tensor(kp[:, k % 2, 2, r], kr[:, k % 2, r], kp[:, k % 2, 1, r],
                                            ALU.subtract).then_inc(sem("parts_ready"), 1)
                if c.values is not None:
                    dve.wait_ge(sem("valued"), c.vj + 1)
                    full = c.rows // P
                    t0 = c.first // P
                    src = ps[:, V_BANK + c.vj % 2, :].rearrange("p (t n) -> p t n", n=P)
                    if c.rows % P:
                        dve.wait_ge(sem("pool"), 3)
                        link(nc.vector.tensor_copy(v_all[0:c.rows % P, t0 + full, :], src[0:c.rows % P, full, :]))
                    nc.vector.tensor_copy(v_all[:, t0:t0 + full, :], src[:, 0:full, :]).then_inc(sem("values_out"), 1)

            def product_out(bank, half, bias, gate, done, value):
                src = ps[:, bank, :].rearrange("p (t n) -> p t n", n=P)
                y, xs = tmp[:, half, :, :], x[:, 4 * half:4 * half + 4, :]
                link(nc.vector.tensor_tensor(y, src, wide[bias][:, :].unsqueeze(1).broadcast_to([P, 4, P]), ALU.add))
                if gate is not None:
                    link(nc.vector.tensor_tensor(y, y, gates[:, gate, :].unsqueeze(1).broadcast_to([P, 4, P]), ALU.mult))
                nc.vector.tensor_tensor(y if bias == "last" else xs, y, xs, ALU.add).then_inc(sem(done), 1)
                dve.wait_ge(sem(done), value)

            def attention(at, v_bias, out_bias, gate):
                S = lambda n: sem(f"{at.name}_{n}")

                def reduce_chunk(h, p, c):
                    n = at.nm * h + c
                    t, c0, width = at.max_chunks[c]
                    dve.wait_ge(S("max_scored"), n + 1)
                    src = ps[:, M_BANK + 2 * ((at.nm * p + c) % 2):M_BANK + 2 * ((at.nm * p + c) % 2) + 2, :]
                    nc.vector.tensor_reduce(max_part[:, t, c0 // MCH:c0 // MCH + 1],
                                            src.rearrange("p b n -> p (b n)")[:, 0:width], AX_X, ALU.max
                                            ).then_inc(S("max_free"), 1)

                def split_max(h, p):
                    dve.wait_ge(S("max_free"), at.nm * h + at.nm - 1 + 2)
                    step = 4 * h
                    nc.vector.tensor_reduce(neg_max[:, :], max_part[:, :, 0:at.per_tile], AX_X, ALU.max,
                                            negate=True).then_inc(S("max_steps"), 1)
                    dve.wait_ge(S("max_steps"), step + 1)
                    nc.vector.tensor_copy(max_parts[:, 0, :], neg_max[:, :]).then_inc(S("max_steps"), 1)
                    dve.wait_ge(S("max_steps"), step + 2)
                    nc.vector.tensor_tensor(max_rest[:, :], neg_max[:, :], max_parts[:, 0, :],
                                            ALU.subtract).then_inc(S("max_steps"), 1)
                    dve.wait_ge(S("max_steps"), step + 3)
                    nc.vector.tensor_copy(max_parts[:, 1, :], max_rest[:, :]).then_inc(S("max_steps"), 1)
                    dve.wait_ge(S("max_steps"), step + 4)
                    nc.vector.tensor_tensor(max_parts[:, 2, :], max_rest[:, :], max_parts[:, 1, :],
                                            ALU.subtract).then_inc(S("max_split"), 1)
                    c = at.nm - 1
                    dve.wait_ge(S("max_scored"), at.nm * h + c + 1)
                    b = M_BANK + 2 * ((at.nm * p + c) % 2)
                    nc.vector.tensor_copy(max_rows[p][:, :], ps[0:PARTS * QT, b, 0:P // 2].bitcast(BF16)
                                          ).then_inc(S("max_free"), 1)

                def whole_max(h, p):
                    for c in range(at.nm - 1):
                        reduce_chunk(h, p, c)
                    split_max(h, p)

                whole_max(0, 0)

                def slot(h, p, has_next, has_next2):
                    if has_next:
                        whole_max(h + 1, 1 - p)
                head_pairs(dve, slot)

                dve.wait_ge(S("sums_loaded"), 64)
                link(nc.vector.tensor_tensor(nd[:, 0, :, :], nd[:, 0, :, :], nd[:, 1, :, :], ALU.add))
                link(nc.vector.reciprocal(nd[:, 1, 1, :], nd[:, 0, 1, :]))
                link(nc.vector.tensor_tensor(nd[:, 1, 0, :], nd[:, 0, 0, :], nd[:, 1, 1, :], ALU.mult))
                nc.vector.tensor_scalar_add(nd[:, 0, 0, :], nd[:, 1, 0, :], v_bias).then_inc(sem("attended"), 1)
                for half in range(2):
                    dve.wait_ge(sem("product_out"), 2 * ATT.index(at.name) + 1 + half)
                    product_out(V_BANK + half, half, out_bias, gate, "tokens_done",
                                2 * ATT.index(at.name) + 1 + half)

            def bias_col(name, k):
                return cols[:, col[name] + k:col[name] + k + 1]

            pipeline("own", normalise, None, project)
            attention(attentions["own"], bias_col("L0_xcond_qkv_b", 2), "self_o", 0)
            pipeline("cross", normalise, None, project)
            attention(attentions["cross"], bias_col("L0_xcond_kv_b", 1), "cross_o", None)
            pipeline("mlp", normalise, None, project)
            pipeline("last", normalise, None, project)
            attention(attentions["last"], bias_col("L1_xcond_bkv", 1), "last", None)

        @block.tensor
        def _(pe):
            pe.wait_ge(sem("rows_loaded"), 16 * len(BIAS_ROWS))
            pe.wait_ge(sem("identities"), 2)
            nc.tensor.transpose(ps[:, 0, 0:NCOL], rows[0:NCOL, :], ident[0:NCOL, 0:NCOL]).then_inc(sem("cols_turned"), 1)
            pe.wait_ge(sem("weights_loaded"), 16 * len(w))
            pe.wait_ge(sem("silu_ready"), 1)
            for k, (name, b, s, _, _) in enumerate(MODS):
                nc.tensor.matmul(ps[:, 1, k:k + 1], w[name][:, b, :], silu[:, 3:4], start=True, stop=True)
                nc.tensor.matmul(ps[:, 1, 4 + k:5 + k], w[name][:, s, :], silu[:, 3:4], start=True, stop=True)
            for k, j in enumerate(GATES):
                last = nc.tensor.matmul(ps[:, 2, k * P:(k + 1) * P], silu_wide[:, :], w["L0_xcond_ada_w"][:, j, :],
                                        start=True, stop=True)
            last.then_inc(sem("mods_product"), 1)
            pe.wait_ge(sem("mods_ready"), 3)

            def turn(c):
                if c.eps is not None:
                    pe.wait_ge(sem("normalised"), c.norm_upto)
                else:
                    pe.wait_ge(sem(f"ctx_loaded{c.load % 2}"), ctx_ready[c.i])
                if c.i >= 2:
                    pe.wait_ge(sem("h_t_ready"), c.i - 1)
                for t, r in enumerate(c.tiles):
                    src = xh[0:r, c.i % 2, t, :] if c.eps is not None else chunk_source(c, t)
                    last = nc.tensor.transpose(ps[:, T_BANK + c.i % 2, t * P:t * P + r], src, ident[0:r, 0:r])
                last.then_inc(sem("turned"), 1)

            def project(c):
                pe.wait_ge(sem("h_t_ready"), c.i + 1)
                src = h_t[:, c.i % 2, 0:c.rows]
                if c.mlp:
                    for f in range(4):
                        k = c.pj + f
                        pe.wait_ge(sem("projected_free"), k - 1)
                        nc.tensor.matmul(ps[:, J_BANK + k % 2, :], w["L0_xcond_mlp_w1"][:, f, :], src,
                                         start=True, stop=True).then_inc(sem("projected"), 1)
                    pe.wait_ge(sem("projected_free"), c.pj + 4)
                    pe.wait_ge(sem("values_out"), c.vj - 1)
                    for t in range(4):
                        for f in range(4):
                            last = nc.tensor.matmul(ps[:, V_BANK + c.vj % 2, t * P:(t + 1) * P],
                                                    hid[:, f, t * P:(t + 1) * P], w["L0_xcond_mlp_w2"][:, f, :],
                                                    start=(f == 0), stop=(f == 3))
                    last.then_inc(sem("valued"), 1)
                    return
                for k, (weights, _, _, _) in zip(range(c.pj, c.pj_upto), c.projections):
                    if k >= 2:
                        pe.wait_ge(sem("projected_free"), k - 1)
                    last = nc.tensor.matmul(ps[:, J_BANK + k % 2, 0:c.rows], weights, src, start=True, stop=True)
                    last.then_inc(sem("projected"), 1)
                if c.values is not None:
                    if c.vj >= 2:
                        pe.wait_ge(sem("values_out"), c.vj - 1)
                    for t, r in enumerate(c.tiles):
                        last = nc.tensor.matmul(ps[0:r, V_BANK + c.vj % 2, t * P:(t + 1) * P],
                                                h_t[:, c.i % 2, t * P:t * P + r], c.values, start=True, stop=True)
                    last.then_inc(sem("valued"), 1)

            def attention(at, weights):
                S = lambda n: sem(f"{at.name}_{n}")

                def max_chunk(h, p, c, loaded):
                    t, c0, width = at.max_chunks[c]
                    if c == 0:
                        pe.wait_ge(S(f"operands{p}"), 16 * at.loads * loaded)
                    pe.wait_ge(S("max_free"), at.nm * h + c + 1)
                    b = M_BANK + 2 * ((at.nm * p + c) % 2)
                    for n in range(0, width, HALF):
                        m = min(HALF, width - n)
                        last = nc.tensor.matmul(ps[:, b + n // HALF, 0:m], qh[p][0:MROW, t * P:(t + 1) * P],
                                                kh[p][0:MROW, c0 + n:c0 + n + m], start=True, stop=True)
                    last.then_inc(S("max_scored"), 1)

                def turn_max(h, p):
                    c = at.nm - 1
                    pe.wait_ge(S("max_split"), h + 1)
                    pe.wait_ge(S("max_free"), at.nm * h + c + 1)
                    b = M_BANK + 2 * ((at.nm * p + c) % 2)
                    nc.tensor.transpose(ps[0:PARTS * QT, b, 0:P // 2].bitcast(BF16),
                                        max_parts[:, :, :].rearrange("p j t -> p (j t)"), ident16[:, :]
                                        ).then_inc(S("max_scored"), 1)

                def score(h, p, u):
                    kt, half = u // 2, u % 2
                    pe.wait_ge(S("exps"), at.units * h + u + 1)
                    nc.tensor.matmul(ps[:, S_BANK + u % 2, :], kh[p][0:KROWS, kt * P:(kt + 1) * P],
                                     qh[p][0:KROWS, half * HALF:(half + 1) * HALF], start=True, stop=True
                                     ).then_inc(S("scored"), 1)

                def values(h, p, b):
                    if b == 0:
                        pe.wait_ge(S("values"), h + 1)
                        pe.wait_ge(S("closed"), h + 1)
                    us = at.batches[b]
                    pe.wait_ge(S("exps"), at.units * h + us[-1] + 1 + 2)
                    for n, u in enumerate(us):
                        g = u % 4
                        last = nc.tensor.matmul(ps[BLOCK * g:BLOCK * g + VW, O_BANK + p, :], vh[p][:, u // 2, :],
                                                probs[:, b % 2, n, :], start=(u < 4), stop=(u + 4 >= at.units))
                    last.then_inc(S("summed"), 1)

                for c in range(at.nm - 1):
                    max_chunk(0, 0, c, 1)
                turn_max(0, 0)
                pe.wait_ge(S("max_loaded0"), 16 * PARTS)
                for u in at.batches[0]:
                    score(0, 0, u)

                def slot(h, p, has_next, loaded):
                    q = 1 - p
                    for b in range(at.nb):
                        chunks = at.chunks_at[b] if has_next else []
                        if b + 1 < at.nb:
                            todo = [(h, p, u) for u in at.batches[b + 1]]
                        elif has_next:
                            pe.wait_ge(S(f"max_loaded{q}"), 16 * PARTS * loaded)
                            todo = [(h + 1, q, u) for u in at.batches[0]]
                        else:
                            todo = []
                        for n, one in enumerate(todo):
                            score(*one)
                            lo, hi = (len(chunks) * k // len(todo) for k in (n, n + 1))
                            for c in chunks[lo:hi]:
                                max_chunk(h + 1, q, c, loaded)
                        if has_next and b == at.turn_at:
                            turn_max(h + 1, q)
                        values(h, p, b)

                with pe.Fori(0, HEADS // 2 - 1) as i:
                    slot(2 * i, 0, True, i + 1)
                    slot(2 * i + 1, 1, True, i + 2)
                slot(HEADS - 2, 0, True, HEADS // 2)
                slot(HEADS - 1, 1, False, None)

                pe.wait_ge(sem("attended"), ATT.index(at.name) + 1)
                for half in range(2):
                    for t in range(4):
                        q0 = (4 * half + t) * P
                        last = nc.tensor.matmul(ps[:, V_BANK + half, t * P:(t + 1) * P], nd[:, 0, 0, q0:q0 + P],
                                                weights, start=True, stop=True)
                    last.then_inc(sem("product_out"), 1)
                if at.name != ATT[-1]:
                    pe.wait_ge(sem("tokens_done"), 2 * ATT.index(at.name) + 2)

            pipeline("own", None, turn, project)
            pe.wait_ge(sem("values_out"), GROUPS["own"][-1].vj_upto)
            attention(attentions["own"], w["L0_xcond_self_o_w"][:, 0, :])
            pipeline("cross", None, turn, project)
            pe.wait_ge(sem("values_out"), GROUPS["cross"][-1].vj_upto)
            attention(attentions["cross"], w["L0_xcond_cross_o_w"][:, 0, :])
            pipeline("mlp", None, turn, project)
            pipeline("last", None, turn, project)
            pe.wait_ge(sem("values_out"), GROUPS["last"][-1].vj_upto)
            attention(attentions["last"], w["L1_xcond_Wp"][:, 0, :])


_INS = ['x', 'cond_1024', 'ctx_1024', 'L0_xcond_ada_w', 'L0_xcond_ada_b', 'L0_xcond_qkv_w', 'L0_xcond_qkv_b',
        'L0_xcond_self_o_w', 'L0_xcond_self_o_b', 'L0_xcond_norm2_g', 'L0_xcond_norm2_b', 'L0_xcond_q_w',
        'L0_xcond_q_b', 'L0_xcond_kv_w', 'L0_xcond_kv_b', 'L0_xcond_cross_o_w', 'L0_xcond_cross_o_b',
        'L0_xcond_mlp_w1', 'L0_xcond_mlp_b1', 'L0_xcond_mlp_w2', 'L0_xcond_mlp_b2', 'L1_xcond_Wq', 'L1_xcond_bq',
        'L1_xcond_Wkv', 'L1_xcond_bkv', 'L1_xcond_Wp', 'L1_xcond_bp', 'L1_xcond_Wss_q', 'L1_xcond_bss_q',
        'L1_xcond_Wss_kv', 'L1_xcond_bss_kv']
_OUT_SHAPE = (1, 1024, 128)


def kernel(**inputs):
    import numpy as _np
    import concourse.bacc as _bacc
    from concourse import mybir as _mybir
    from concourse.bass_utils import run_bass_kernel_spmd as _run

    nc = _bacc.Bacc("TRN2", target_bir_lowering=False, num_devices=1)
    arrays, aps = {}, {}
    for name in _INS:
        v = _np.ascontiguousarray(inputs[name])
        arrays[f"in_{name}"] = v
        aps[name] = nc.dram_tensor(f"in_{name}", v.shape, _mybir.dt.from_np(v.dtype), kind="ExternalInput").ap()
    out = nc.dram_tensor("out_0", _OUT_SHAPE, _mybir.dt.float32, kind="ExternalOutput").ap()
    pixart_program(nc, aps, out)
    r = _run(nc, [arrays], core_ids=[0])
    return r.results[0]["out_0"]
```

```python
from contextlib import ExitStack

import concourse.bass as bass
from concourse import mybir

ALU = mybir.AluOpType
ACT = mybir.ActivationFunctionType
AX_X = mybir.AxisListType.X
F32 = mybir.dt.float32
BF16 = mybir.dt.bfloat16

P = 128
HEADS = 16
DH = P // HEADS
QN = 1024
QT = QN // P
HALF = 512
CTX = 6404
SCALE = float(DH) ** -0.5
PARTS = 3
BLOCK = 32
MROW = PARTS * BLOCK
KROWS = MROW + PARTS
VW = 32
MCH = 1024


def ceil_div(a, b):
    return -(-a // b)


def batches(units):
    return [list(range(u, min(u + 4, units))) for u in range(0, units, 4)]


class Attention:

    def __init__(self, name, keys, ahead, turn):
        self.name, self.keys, self.ahead = name, keys, ahead
        self.kt = ceil_div(keys, P)
        self.units = 2 * self.kt
        self.batches = batches(self.units)
        self.nb = len(self.batches)
        self.lookahead = 1 if self.nb < 8 else 3
        self.max_chunks = [(t, c, min(MCH, keys - c)) for c in range(0, keys, MCH) for t in range(QT)]
        self.per_tile = ceil_div(keys, MCH)
        n = len(self.max_chunks)
        chunks = lambda dh, a, b: [("chunk", dh, c) for c in range(a, b)]
        following = lambda dh: chunks(dh + 1, 0, turn) + [("turn", dh, None)] + chunks(dh + 1, turn, ahead)
        self.first = chunks(0, 0, n) + following(0)
        self.beside = chunks(1, ahead, n) + following(1)
        self.beside_last = chunks(1, ahead, n) + [("turn", 1, None)]
        self.first_turn = self.first.index(("turn", 0, None))
        self.turn = self.beside.index(("turn", 1, None))
        self.last_turn = self.beside_last.index(("turn", 1, None))
        self.small = 2 * keys <= CTX
        self.max_keys = keys if self.small else 0
        self.pieces = [(0, self.kt)] if self.small else [(a, min(a + 13, self.kt)) for a in range(0, self.kt, 13)]
        assert self.turn < len(self.beside) * (self.nb - 1) // self.nb
        assert self.nb % 2 == 0 and self.nb > self.lookahead and ahead <= QT

    def number(self, h, e):
        return len(self.first) + len(self.beside) * h + e

    def events_at(self, b, events):
        n = len(self.beside)
        return [(e, events[e]) for e in range(n * b // self.nb, n * (b + 1) // self.nb) if e < len(events)]


class Chunk:

    def __init__(self, source, first, rows, eps, scale, shift, projections=(), values=None, mlp=False):
        self.source, self.first, self.rows, self.eps = source, first, rows, eps
        self.scale, self.shift = scale, shift
        self.projections, self.values, self.mlp = projections, values, mlp
        self.tiles = [min(P, rows - a) for a in range(0, rows, P)]


BIAS_ROWS = ["L0_xcond_ada_b", "L0_xcond_qkv_b", "L0_xcond_norm2_g", "L0_xcond_norm2_b", "L0_xcond_q_b",
             "L0_xcond_kv_b", "L0_xcond_mlp_b1", "L1_xcond_bq", "L1_xcond_bkv", "L1_xcond_bss_q",
             "L1_xcond_bss_kv", "cond_1024"]


def pixart_program(nc, a, out):
    col, n = {}, 0
    for name in BIAS_ROWS:
        size = 1
        for s in a[name].shape:
            size *= s
        col[name] = n
        n += size // P
    NCOL = n

    attentions = {"own": Attention("own", QN, 6, 1), "cross": Attention("cross", CTX, 8, 2),
                  "last": Attention("last", CTX, 8, 2)}

    dram = {}
    for n, at in attentions.items():
        dram[n, "q"] = nc.dram_tensor(f"{n}_q_parts", (PARTS, P, QN), BF16, kind="Internal").ap()
        dram[n, "k"] = nc.dram_tensor(f"{n}_k_parts", (PARTS, P, at.keys), BF16, kind="Internal").ap()
        dram[n, "o"] = nc.dram_tensor(f"{n}_heads_out", (2, 2, P, QN), F32, kind="Internal").ap()

    with ExitStack() as ctx:
        def sb(name, shape, dt=F32):
            return ctx.enter_context(nc.sbuf_tensor(name, shape, dt))

        sems = {}

        def sem(name):
            if name not in sems:
                sems[name] = ctx.enter_context(nc.semaphore(name))
            return sems[name]

        ps = ctx.enter_context(nc.psum_tensor("ps", [P, 8, HALF], F32))
        S_BANK, O_BANK, M_BANK = 0, 2, 4
        T_BANK, J_BANK, V_BANK = 0, 2, 4

        KTILES = attentions["cross"].kt
        kh = [sb(f"kh{i}", [P, KTILES * P], BF16) for i in range(2)]
        qh = [sb(f"qh{i}", [P, QN], BF16) for i in range(2)]
        qm = [sb(f"qm{i}", [P, QN], BF16) for i in range(2)]
        v_all = sb("v_all", [P, KTILES, P])
        vh = [sb(f"vh{i}", [P, KTILES, VW]) for i in range(2)]
        probs = sb("probs", [P, 2, 4, HALF])
        mark = sb("mark", [P, 1])
        mark_dram = nc.dram_tensor("mark_stored", (len(attentions), P, 1), F32, kind="Internal").ap()
        heads_out = [sb(f"heads_out{i}", [P, HALF]) for i in range(2)]
        max_part = [sb(f"max_part{i}", [P, QT, ceil_div(CTX, MCH)]) for i in range(2)]
        neg_max = sb("neg_max", [P, QT])
        max_rest = sb("max_rest", [P, QT])
        max_parts = sb("max_parts", [P, PARTS, QT], BF16)
        max_rows = [sb(f"max_rows{i}", [PARTS * QT, P], BF16) for i in range(2)]
        nd = sb("nd", [P, 2, 2, QN])
        x = sb("x", [P, QT, P])
        nat = sb("nat", [P, 2, 4, P])
        xh = sb("xh", [P, 2, 4, P])
        h_t = sb("h_t", [P, 2, HALF])
        kf = sb("kf", [P, 2, HALF])
        kr = sb("kr", [P, 2, HALF])
        kp = sb("kp", [P, 2, PARTS, HALF], BF16)
        hid = sb("hid", [P, 4, HALF])
        tmp = sb("tmp", [P, 2, 4, P])
        stats = sb("stats", [P, 4, 6])
        mv = sb("mv", [P, 4, 2])
        sd = sb("sd", [P, 4])
        rstd = sb("rstd", [P, 4])
        ident = sb("ident", [P, P])
        ident16 = sb("ident16", [P, P], BF16)
        rows = sb("rows", [P, P])
        cols = sb("cols", [P, NCOL])
        one_cols = sb("one_cols", [P, 2])
        credits = sb("credits", [P, 16])
        silu = sb("silu", [P, 4])
        silu_wide = sb("silu_wide", [P, P])
        shifts = sb("shifts", [P, 8])
        scales = sb("scales", [P, 8])
        gates = sb("gates", [P, 2, P])
        wide = {n: sb(f"wide_{n}", [P, P]) for n in ("gate0", "gate1", "self_o", "cross_o", "mlp", "last")}

        w = {}
        for n, width in (("L0_xcond_ada_w", 6), ("L0_xcond_qkv_w", 3), ("L0_xcond_self_o_w", 1), ("L0_xcond_q_w", 1),
                         ("L0_xcond_kv_w", 2), ("L0_xcond_cross_o_w", 1), ("L0_xcond_mlp_w1", 4),
                         ("L0_xcond_mlp_w2", 4), ("L1_xcond_Wq", 1), ("L1_xcond_Wkv", 2), ("L1_xcond_Wp", 1),
                         ("L1_xcond_Wss_q", 2), ("L1_xcond_Wss_kv", 2)):
            w[n] = sb("w_" + n, [P, width, P])

        x_dram = a["x"].rearrange("o (t p) c -> p (o t) c", p=P)
        out_dram = out.rearrange("o (t p) c -> p (o t) c", p=P)
        ctx_dram = a["ctx_1024"].rearrange("o n c -> (o n) c")

        MSA, MLP, SSQ, SSKV = 0, 1, 2, 3
        ab, bq, bk = col["L0_xcond_ada_b"], col["L1_xcond_bss_q"], col["L1_xcond_bss_kv"]
        MODS = [("L0_xcond_ada_w", 0, 1, ab + 0, ab + 1), ("L0_xcond_ada_w", 3, 4, ab + 3, ab + 4),
                ("L1_xcond_Wss_q", 1, 0, bq + 1, bq + 0), ("L1_xcond_Wss_kv", 1, 0, bk + 1, bk + 0)]
        GATES = [2, 5]

        def mod(k):
            return scales[:, k:k + 1], shifts[:, k:k + 1]

        norm2 = (cols[:, col["L0_xcond_norm2_g"]:col["L0_xcond_norm2_g"] + 1],
                 cols[:, col["L0_xcond_norm2_b"]:col["L0_xcond_norm2_b"] + 1])
        plain = (one_cols[:, 0:1], one_cols[:, 1:2])

        def proj(weights, k, bias, k2, dst, first):
            c = col[bias] + k2
            return (w[weights][:, k, :], cols[:, c:c + 1], dst, first)

        def token_chunks(make):
            return [make(f) for f in range(0, QN, HALF)]

        def ctx_chunks(make):
            return [make(f, min(HALF, CTX - f)) for f in range(0, CTX, HALF)]

        GROUPS = {
            "own": token_chunks(lambda f: Chunk(
                "x", f, HALF, 1e-6, *mod(MSA),
                [proj("L0_xcond_qkv_w", 0, "L0_xcond_qkv_b", 0, dram["own", "q"], f),
                 proj("L0_xcond_qkv_w", 1, "L0_xcond_qkv_b", 1, dram["own", "k"], f)],
                w["L0_xcond_qkv_w"][:, 2, :])),
            "cross": ctx_chunks(lambda f, r: Chunk(
                "ctx", f, r, None, *plain,
                [proj("L0_xcond_kv_w", 0, "L0_xcond_kv_b", 0, dram["cross", "k"], f)],
                w["L0_xcond_kv_w"][:, 1, :]))
            + token_chunks(lambda f: Chunk(
                "x", f, HALF, 1e-6, *norm2,
                [proj("L0_xcond_q_w", 0, "L0_xcond_q_b", 0, dram["cross", "q"], f)])),
            "mlp": token_chunks(lambda f: Chunk("x", f, HALF, 1e-6, *mod(MLP), mlp=True)),
            "last": ctx_chunks(lambda f, r: Chunk(
                "ctx", f, r, 1e-5, *mod(SSKV),
                [proj("L1_xcond_Wkv", 0, "L1_xcond_bkv", 0, dram["last", "k"], f)],
                w["L1_xcond_Wkv"][:, 1, :]))
            + token_chunks(lambda f: Chunk(
                "x", f, HALF, 1e-5, *mod(SSQ),
                [proj("L1_xcond_Wq", 0, "L1_xcond_bq", 0, dram["last", "q"], f)])),
        }
        ORDER = ["own", "cross", "mlp", "last"]

        all_chunks = [c for g in ORDER for c in GROUPS[g]]
        loads, ln, pj, vj, mo = 0, 0, 0, 0, 0
        for i, c in enumerate(all_chunks):
            c.i = i
            c.load = loads
            loads += c.source == "ctx"
            c.norm = ln
            ln += c.eps is not None
            c.norm_upto = ln
            c.pj = pj
            pj += len(c.projections) + (4 if c.mlp else 0)
            c.pj_upto = pj
            c.vj = vj
            vj += c.values is not None or c.mlp
            c.vj_upto = vj
        stored = {}
        n_store = [0, 0]
        for c in all_chunks:
            if not c.mlp:
                for k in range(c.pj, c.pj_upto):
                    stored[k] = n_store[k % 2]
                    n_store[k % 2] += 1
        stores_upto = {}
        run = [0, 0]
        for g in ORDER:
            for c in GROUPS[g]:
                if not c.mlp:
                    for k in range(c.pj, c.pj_upto):
                        run[k % 2] += 1
            stores_upto[g] = tuple(run)

        k_ready, n = {}, 0
        for c in all_chunks:
            if not c.mlp:
                for k in range(c.pj, c.pj_upto):
                    n += 1
                    k_ready[k] = n
        ctx_ready, n = {}, [0, 0]
        for c in all_chunks:
            if c.source == "ctx":
                n[c.load % 2] += 16 * (1 + (c.rows % P > 0))
                ctx_ready[c.i] = n[c.load % 2]
        ATT = list(attentions)

        def pipeline(group, normalise, turn, project):
            g = GROUPS[group]
            for s in range(-2, len(g)):
                if normalise and s + 2 < len(g):
                    normalise(g[s + 2])
                if turn and 0 <= s + 1 < len(g):
                    turn(g[s + 1])
                if project and s >= 0:
                    project(g[s])

        def chunk_source(c, t):
            if c.source == "x":
                return x[0:c.tiles[t], c.first // P + t, :]
            return nat[0:c.tiles[t], c.load % 2, t, :]

        def head_pairs(eng, slot):
            with eng.Fori(0, HEADS // 2 - 1) as i:
                slot(2 * i, 0, True, True)
                slot(2 * i + 1, 1, True, True)
            slot(HEADS - 2, 0, True, False)
            slot(HEADS - 1, 1, False, False)

        block = ctx.enter_context(nc.Block())

        @block.sync
        def _(sp):
            for name in BIAS_ROWS:
                v = a[name]
                v = v.rearrange("o (r p) -> (o r) p", p=P) if len(v.shape) == 2 else v.rearrange("(r p) -> r p", p=P)
                sp.dma_start(rows[col[name]:col[name] + v.shape[0], :], v).then_inc(sem("rows_loaded"), 16)
            sp.dma_start(x[:, :, :], x_dram).then_inc(sem("x_loaded"), 16)
            for name, t in w.items():
                src = a[name].rearrange("(t p) n -> p t n", p=P) if name == "L0_xcond_mlp_w2" else \
                    a[name].rearrange("p (t n) -> p t n", n=P)
                sp.dma_start(t[:, :, :], src).then_inc(sem("weights_loaded"), 16)
            for n, v in (("gate0", a["L0_xcond_ada_b"][2 * P:3 * P]), ("gate1", a["L0_xcond_ada_b"][5 * P:6 * P]),
                         ("self_o", a["L0_xcond_self_o_b"]), ("cross_o", a["L0_xcond_cross_o_b"]),
                         ("mlp", a["L0_xcond_mlp_b2"]), ("last", a["L1_xcond_bp"])):
                sp.dma_start(wide[n][:, :], v.partition_broadcast(P)).then_inc(sem("wide_loaded"), 16)

            def load_ctx(c):
                if c.source != "ctx":
                    return
                if c.load >= 2:
                    prev = next(d for d in all_chunks if d.source == "ctx" and d.load == c.load - 2)
                    if prev.eps is not None:
                        sp.wait_ge(sem("normalised"), prev.norm_upto)
                    else:
                        sp.wait_ge(sem("turned"), prev.i + 1)
                s = sem(f"ctx_loaded{c.load % 2}")
                full = c.rows // P
                sp.dma_start(nat[:, c.load % 2, 0:full, :],
                             ctx_dram[c.first:c.first + full * P, :].rearrange("(t p) n -> p t n", p=P)).then_inc(s, 16)
                if c.rows % P:
                    sp.dma_start(nat[0:c.rows % P, c.load % 2, full, :],
                                 ctx_dram[c.first + full * P:c.first + c.rows, :]).then_inc(s, 16)

            def store_parts(c):
                if c.mlp:
                    return
                for k, (_, _, dst, first) in zip(range(c.pj, c.pj_upto), c.projections):
                    sp.wait_ge(sem("parts_ready"), k_ready[k])
                    sp.dma_start(dst[:, :, first:first + c.rows].rearrange("j f n -> f j n"),
                                 kp[:, k % 2, :, 0:c.rows]).then_inc(sem(f"parts_stored{k % 2}"), 16)

            def chunk_transfers(group):
                g = GROUPS[group]
                for s in range(-3, len(g)):
                    if s + 3 < len(g):
                        load_ctx(g[s + 3])
                    if s >= 0:
                        store_parts(g[s])

            def attention(at):
                S = lambda n: sem(f"{at.name}_{n}")
                q_parts, k_parts, o_dram = (dram[at.name, n] for n in "qko")

                def load_keys(h, p, j0, behind, signal):
                    c0, c1 = at.pieces[j0][0] * P, min(at.pieces[j0][1] * P, at.keys)
                    for j in range(PARTS):
                        sp.dma_start(kh[p][BLOCK * j:BLOCK * j + PARTS * DH, behind + c0:behind + c1],
                                     k_parts[j, bass.ds(h * DH, DH), c0:c1].unsqueeze(0)
                                     .broadcast_to([PARTS, DH, c1 - c0])).then_inc(S(signal), 16)

                def load_queries(h, p, to, signal):
                    for j in range(PARTS):
                        sp.dma_start(to[p][BLOCK * j:BLOCK * j + PARTS * DH, :],
                                     q_parts[:, bass.ds(h * DH, DH), :]).then_inc(S(signal), 16)

                def load_for_max(h, p):
                    load_queries(h, p, qm, f"for_max{p}")
                    if at.small:
                        load_keys(h, p, 0, at.max_keys, f"for_max{p}")

                def store_max(p, number, heads_before):
                    sp.wait_ge(S("max_free"), number + 1 + 2)
                    for j in range(PARTS):
                        if j == PARTS - 1:
                            sp.wait_ge(S("heads_stored"), 4 * 16 * heads_before + 16)
                        sp.dma_start(qh[p][MROW + j:MROW + j + 1, :].rearrange("o (t q) -> o t q", q=P),
                                     max_rows[p][QT * j:QT * (j + 1), :]).then_inc(S(f"max_loaded{p}"), 16)

                for k, n in enumerate(stores_upto[at.name]):
                    sp.wait_ge(sem(f"parts_stored{k}"), 16 * n)
                sp.wait_ge(sem("zeroed"), 1)
                for h in range(2):
                    load_for_max(h, h)
                    if at.small and h == 1:
                        continue
                    for j in range(len(at.pieces)):
                        load_keys(h, h, j, 0, f"keys{h}_{j}")
                    load_queries(h, h, qh, f"queries{h}")
                store_max(0, at.first_turn, 0)

                def slot_small(h, p, has_next, has_next2):
                    if has_next2:
                        sp.wait_ge(S("max_scored"), at.number(h, 0) - len(at.beside) + len(at.max_chunks) - at.ahead)
                        load_for_max(h + 2, p)
                    if has_next:
                        sp.wait_ge(S("scored"), at.units * h + 1)
                        load_queries(h + 1, 1 - p, qh, f"queries{1 - p}")
                        load_keys(h + 1, 1 - p, 0, 0, f"keys{1 - p}_0")
                        store_max(1 - p, at.number(h, at.turn if has_next2 else at.last_turn), h)

                def slot(h, p, has_next, has_next2):
                    if has_next2:
                        sp.wait_ge(S("max_scored"), at.number(h, 0))
                        load_for_max(h + 2, p)
                        for j, piece in enumerate(at.pieces[:-1]):
                            sp.wait_ge(S("scored"), at.units * h + 2 * piece[1])
                            load_keys(h + 2, p, j, 0, f"keys{p}_{j}")
                    if has_next:
                        store_max(1 - p, at.number(h, at.turn if has_next2 else at.last_turn), h)
                    if has_next2:
                        sp.wait_ge(S("scored"), at.units * (h + 1))
                        load_queries(h + 2, p, qh, f"queries{p}")
                        j = len(at.pieces) - 1
                        load_keys(h + 2, p, j, 0, f"keys{p}_{j}")
                head_pairs(sp, slot_small if at.small else slot)
                sp.wait_ge(S("heads_stored"), 4 * 16 * HEADS + 16)
                for g in range(2):
                    for n in range(2):
                        sp.dma_start(nd[:, g, n, :], o_dram[g, n, :, :]).then_inc(S("sums_loaded"), 16)

            chunk_transfers("own")
            attention(attentions["own"])
            chunk_transfers("cross")
            attention(attentions["cross"])
            chunk_transfers("last")
            attention(attentions["last"])
            for t in range(2):
                sp.wait_ge(sem("tokens_done"), 2 * len(ATT) - 1 + t)
                sp.dma_start(out_dram[:, 4 * t:4 * t + 4, :], tmp[:, t, :, :]).then_inc(sem("out_stored"), 16)
            sp.wait_ge(sem("out_stored"), 32)

        @block.gpsimd
        def _(pool):
            nc.gpsimd.memset(ident[:, :], 0.0).then_inc(sem("pool"), 1)
            nc.gpsimd.memset(ident16[:, :], 0.0).then_inc(sem("pool"), 1)
            nc.gpsimd.memset(mark[:, :], 0.0).then_inc(sem("pool"), 1)
            pool.wait_ge(sem("pool"), 3)
            for t in (ident, ident16):
                nc.gpsimd.affine_select(out=t[:, :], in_=t[:, :], compare_op=ALU.not_equal, fill=1.0, base=0,
                                        pattern=[[-1, P]], channel_multiplier=1).then_inc(sem("identities"), 1)
            nc.gpsimd.memset(v_all[:, KTILES - 1, :], 0.0).then_inc(sem("pool"), 1)
            for i in range(2):
                nc.gpsimd.memset(vh[i][:, :, :], 0.0).then_inc(sem("pool"), 1)
            pool.wait_ge(sem("pool"), 6)
            for i in range(2):
                nc.gpsimd.memset(vh[i][:, 0:KTILES - 1, DH:2 * DH], 1.0).then_inc(sem("pool"), 1)
                nc.gpsimd.memset(vh[i][0:CTX % P, KTILES - 1, DH:2 * DH], 1.0).then_inc(sem("pool"), 1)
            pool.wait_ge(sem("pool"), 10)

            def attention(at, vj):
                S = lambda n: sem(f"{at.name}_{n}")
                o_dram = dram[at.name, "o"]

                def copy_values(h, p):
                    nc.gpsimd.tensor_copy(vh[p][:, 0:at.kt, 0:DH], v_all[:, 0:at.kt, bass.ds(h * DH, DH)]
                                          ).then_inc(S("values"), 1)
                pool.dma_start(mark_dram[ATT.index(at.name), :, :], mark[:, :]).then_inc(S("heads_stored"), 16)
                pool.wait_ge(sem("values_out"), vj)
                copy_values(0, 0)
                copy_values(1, 1)

                def slot(h, p, has_next, has_next2):
                    if has_next2:
                        pool.wait_ge(S("summed"), at.nb * (h + 1) + 2)
                        copy_values(h + 2, p)
                    pool.wait_ge(S("closed"), h + 1 + 2)
                    for g in range(4):
                        pool.dma_start(o_dram[g // 2, :, bass.ds(h * DH, DH), (g % 2) * HALF:(g % 2 + 1) * HALF],
                                     heads_out[p][BLOCK * g:BLOCK * g + 2 * DH, :]).then_inc(S("heads_stored"), 16)
                head_pairs(pool, slot)

            attention(attentions["own"], GROUPS["own"][-1].vj_upto)
            attention(attentions["cross"], GROUPS["cross"][-1].vj_upto)
            attention(attentions["last"], GROUPS["last"][-1].vj_upto)

        @block.scalar
        def _(act):
            act.wait_ge(sem("cols_ready"), 1)
            cc = col["cond_1024"]
            nc.scalar.activation(silu[:, 0:1], cols[:, cc:cc + 1], ACT.Exp, scale=-1.0).then_inc(sem("cond_exp"), 1)

            def root(c):
                if c.eps is None:
                    return
                act.wait_ge(sem("variances"), c.norm_upto)
                r = c.tiles[0]
                nc.scalar.activation(sd[0:r, 0:len(c.tiles)], sd[0:r, 0:len(c.tiles)], ACT.Sqrt).then_inc(sem("roots"), 1)

            def evacuate_turned(c):
                act.wait_ge(sem("turned"), c.i + 1)
                if c.i == 0:
                    act.wait_ge(sem("mods_ready"), 3)
                if c.i >= 2:
                    old = all_chunks[c.i - 2]
                    if old.values is not None:
                        act.wait_ge(sem("valued"), old.vj_upto)
                    else:
                        act.wait_ge(sem("projected"), old.pj_upto)
                nc.scalar.activation(h_t[:, c.i % 2, 0:c.rows], ps[:, T_BANK + c.i % 2, 0:c.rows], ACT.Identity,
                                     bias=c.shift, scale=c.scale).then_inc(sem("h_t_ready"), 1)

            def evacuate_projected(c):
                if c.mlp:
                    for f in range(4):
                        act.wait_ge(sem("projected"), c.pj + f + 1)
                        if f == 0 and c.vj > GROUPS["mlp"][0].vj:
                            act.wait_ge(sem("valued"), c.vj)
                        b1 = col["L0_xcond_mlp_b1"] + f
                        nc.scalar.activation(hid[:, f, :], ps[:, J_BANK + (c.pj + f) % 2, :], ACT.Gelu_apprx_tanh,
                                             bias=cols[:, b1:b1 + 1]).then_inc(sem("projected_free"), 1)
                    return
                for k, (_, bias, _, _) in zip(range(c.pj, c.pj_upto), c.projections):
                    act.wait_ge(sem("projected"), k + 1)
                    if stored[k]:
                        act.wait_ge(sem(f"parts_stored{k % 2}"), 16 * stored[k])
                    src = ps[:, J_BANK + k % 2, 0:c.rows]
                    nc.scalar.activation(kf[:, k % 2, 0:c.rows], src, ACT.Identity, bias=bias).then_inc(sem("kf_ready"), 1)
                    nc.scalar.activation(kp[:, k % 2, 0, 0:c.rows], src, ACT.Identity, bias=bias).then_inc(sem("projected_free"), 1)

            def attention(at):
                S = lambda n: sem(f"{at.name}_{n}")

                def exps(h, b):
                    act.wait_ge(S("summed"), at.nb * h + b + 1)
                    for n, u in enumerate(at.batches[b]):
                        act.wait_ge(S("scored"), at.units * h + u + 1)
                        nc.scalar.activation(probs[:, b % 2, n, :], ps[:, S_BANK + u % 2, :], ACT.Exp,
                                             scale=SCALE).then_inc(S("exps"), 1)

                def close(h, p):
                    act.wait_ge(S("summed"), at.nb * (h + 1) + 2)
                    nc.scalar.activation(heads_out[p][:, :], ps[:, O_BANK + p, :], ACT.Copy).then_inc(S("closed"), 1)

                for b in range(at.lookahead):
                    exps(0, b)

                def slot(h, p, has_next, has_next2):
                    for b in range(at.lookahead, at.nb):
                        exps(h, b)
                    if has_next:
                        for b in range(at.lookahead):
                            exps(h + 1, b)
                    close(h, p)
                head_pairs(act, slot)

            pipeline("own", root, evacuate_turned, evacuate_projected)
            attention(attentions["own"])
            pipeline("cross", root, evacuate_turned, evacuate_projected)
            attention(attentions["cross"])
            pipeline("mlp", root, evacuate_turned, evacuate_projected)
            pipeline("last", root, evacuate_turned, evacuate_projected)
            attention(attentions["last"])

        @block.vector
        def _(dve):
            chain = [0]

            def link(ins):
                chain[0] += 1
                ins.then_inc(sem("dve_chain"), 1)
                dve.wait_ge(sem("dve_chain"), chain[0])

            for i in range(2):
                link(nc.vector.memset(kh[i][:, :], 0.0))
                link(nc.vector.memset(kh[i][MROW:KROWS, 0:CTX], 1.0))
                link(nc.vector.memset(qh[i][:, :], 0.0))
                link(nc.vector.memset(qm[i][:, :], 0.0))
            link(nc.vector.memset(one_cols[:, 0:1], 1.0))
            nc.vector.memset(one_cols[:, 1:2], 0.0).then_inc(sem("zeroed"), 1)
            credit = iter(range(16))
            for at in attentions.values():
                for n, places in (("exps", 2), ("max_free", 2), ("summed", 2), ("closed", 2)):
                    k = next(credit)
                    nc.vector.memset(credits[:, k:k + 1], 0.0).then_inc(sem(f"{at.name}_{n}"), places)

            dve.wait_ge(sem("cols_turned"), 1)
            nc.vector.tensor_copy(cols[:, :], ps[:, 0, 0:NCOL]).then_inc(sem("cols_ready"), 1)
            dve.wait_ge(sem("cols_ready"), 1)
            dve.wait_ge(sem("cond_exp"), 1)
            cc = col["cond_1024"]
            link(nc.vector.tensor_scalar_add(silu[:, 1:2], silu[:, 0:1], 1.0))
            link(nc.vector.reciprocal(silu[:, 2:3], silu[:, 1:2]))
            link(nc.vector.tensor_tensor(silu[:, 3:4], silu[:, 2:3], cols[:, cc:cc + 1], ALU.mult))
            nc.vector.tensor_copy(silu_wide[:, :], silu[:, 3:4].broadcast_to([P, P])).then_inc(sem("silu_ready"), 1)
            dve.wait_ge(sem("mods_product"), 1)
            for k, (_, _, _, cb, cs) in enumerate(MODS):
                link(nc.vector.tensor_tensor(shifts[:, k:k + 1], ps[:, 1, k:k + 1], cols[:, cb:cb + 1], ALU.add))
                link(nc.vector.tensor_tensor(scales[:, 4 + k:5 + k], ps[:, 1, 4 + k:5 + k], cols[:, cs:cs + 1], ALU.add))
            nc.vector.tensor_scalar_add(scales[:, 0:4], scales[:, 4:8], 1.0).then_inc(sem("mods_ready"), 1)
            dve.wait_ge(sem("wide_loaded"), 16 * len(wide))
            for k in range(2):
                nc.vector.tensor_tensor(gates[:, k, :], ps[:, 2, k * P:(k + 1) * P], wide[f"gate{k}"][:, :],
                                        ALU.add).then_inc(sem("mods_ready"), 1)

            def normalise(c):
                if c.eps is None:
                    return
                if c.source == "ctx":
                    dve.wait_ge(sem(f"ctx_loaded{c.load % 2}"), ctx_ready[c.i])
                elif c.i == 0:
                    dve.wait_ge(sem("x_loaded"), 16)
                if c.i >= 2:
                    dve.wait_ge(sem("turned"), c.i - 1)
                for t, r in enumerate(c.tiles):
                    last = nc.vector.bn_stats(stats[0:r, t, :], chunk_source(c, t))
                    last.then_inc(sem("dve_chain"), 1)
                    chain[0] += 1
                dve.wait_ge(sem("dve_chain"), chain[0])
                for t, r in enumerate(c.tiles):
                    nc.vector.bn_aggr(mv[0:r, t, :], stats[0:r, t, :]).then_inc(sem("dve_chain"), 1)
                    chain[0] += 1
                dve.wait_ge(sem("dve_chain"), chain[0])
                n_full = sum(r == P for r in c.tiles)
                if c.tiles[-1] != P:
                    link(nc.vector.memset(sd[:, n_full:n_full + 1], 1.0))
                    link(nc.vector.tensor_scalar_add(sd[0:c.tiles[-1], n_full:n_full + 1],
                                                     mv[0:c.tiles[-1], n_full, 1:2], c.eps))
                nc.vector.tensor_scalar_add(sd[:, 0:n_full], mv[:, 0:n_full, 1], c.eps).then_inc(sem("variances"), 1)
                dve.wait_ge(sem("roots"), c.norm_upto)
                link(nc.vector.reciprocal(rstd[:, 0:len(c.tiles)], sd[:, 0:len(c.tiles)]))
                for t, r in enumerate(c.tiles):
                    last = nc.vector.tensor_scalar(xh[0:r, c.i % 2, t, :], chunk_source(c, t), mv[0:r, t, 0:1],
                                                   rstd[0:r, t:t + 1], ALU.subtract, ALU.mult)
                last.then_inc(sem("normalised"), 1)

            def project(c):
                if c.mlp:
                    half = c.first // HALF
                    dve.wait_ge(sem("valued"), c.vj + 1)
                    product_out(V_BANK + c.vj % 2, half, "mlp", 1, "values_out", c.vj + 1)
                    return
                for k in range(c.pj, c.pj_upto):
                    dve.wait_ge(sem("kf_ready"), k_ready[k])
                    dve.wait_ge(sem("projected_free"), k + 1)
                    r = slice(0, c.rows)
                    link(nc.vector.tensor_tensor(kr[:, k % 2, r], kf[:, k % 2, r], kp[:, k % 2, 0, r], ALU.subtract))
                    link(nc.vector.tensor_copy(kp[:, k % 2, 1, r], kr[:, k % 2, r]))
                    nc.vector.tensor_tensor(kp[:, k % 2, 2, r], kr[:, k % 2, r], kp[:, k % 2, 1, r],
                                            ALU.subtract).then_inc(sem("parts_ready"), 1)
                if c.values is not None:
                    dve.wait_ge(sem("valued"), c.vj + 1)
                    full = c.rows // P
                    t0 = c.first // P
                    src = ps[:, V_BANK + c.vj % 2, :].rearrange("p (t n) -> p t n", n=P)
                    if c.rows % P:
                        dve.wait_ge(sem("pool"), 4)
                        link(nc.vector.tensor_copy(v_all[0:c.rows % P, t0 + full, :], src[0:c.rows % P, full, :]))
                    nc.vector.tensor_copy(v_all[:, t0:t0 + full, :], src[:, 0:full, :]).then_inc(sem("values_out"), 1)

            def product_out(bank, half, bias, gate, done, value):
                src = ps[:, bank, :].rearrange("p (t n) -> p t n", n=P)
                y, xs = tmp[:, half, :, :], x[:, 4 * half:4 * half + 4, :]
                link(nc.vector.tensor_tensor(y, src, wide[bias][:, :].unsqueeze(1).broadcast_to([P, 4, P]), ALU.add))
                if gate is not None:
                    link(nc.vector.tensor_tensor(y, y, gates[:, gate, :].unsqueeze(1).broadcast_to([P, 4, P]), ALU.mult))
                nc.vector.tensor_tensor(y if bias == "last" else xs, y, xs, ALU.add).then_inc(sem(done), 1)
                dve.wait_ge(sem(done), value)

            def attention(at, v_bias, out_bias, gate):
                S = lambda n: sem(f"{at.name}_{n}")

                def place(number):
                    return M_BANK + 2 * (number % 2)

                def reduce_chunk(number, odd, h, p, c):
                    t, c0, width = at.max_chunks[c]
                    dve.wait_ge(S("max_scored"), number + 1)
                    src = ps[:, place(odd):place(odd) + 2, :].rearrange("p b n -> p (b n)")
                    nc.vector.tensor_reduce(max_part[p][:, t, c0 // MCH:c0 // MCH + 1], src[:, 0:width], AX_X,
                                            ALU.max).then_inc(S("max_free"), 1)
                    if c == len(at.max_chunks) - 1:
                        split_max(number, h, p)

                def split_max(number, h, p):
                    dve.wait_ge(S("max_free"), number + 1 + 2)
                    step = 4 * h
                    nc.vector.tensor_reduce(neg_max[:, :], max_part[p][:, :, 0:at.per_tile], AX_X, ALU.max,
                                            negate=True).then_inc(S("max_steps"), 1)
                    dve.wait_ge(S("max_steps"), step + 1)
                    nc.vector.tensor_copy(max_parts[:, 0, :], neg_max[:, :]).then_inc(S("max_steps"), 1)
                    dve.wait_ge(S("max_steps"), step + 2)
                    nc.vector.tensor_tensor(max_rest[:, :], neg_max[:, :], max_parts[:, 0, :],
                                            ALU.subtract).then_inc(S("max_steps"), 1)
                    dve.wait_ge(S("max_steps"), step + 3)
                    nc.vector.tensor_copy(max_parts[:, 1, :], max_rest[:, :]).then_inc(S("max_steps"), 1)
                    dve.wait_ge(S("max_steps"), step + 4)
                    nc.vector.tensor_tensor(max_parts[:, 2, :], max_rest[:, :], max_parts[:, 1, :],
                                            ALU.subtract).then_inc(S("max_split"), 1)

                def keep_turned(number, odd, p):
                    dve.wait_ge(S("max_scored"), number + 1)
                    nc.vector.tensor_copy(max_rows[p][:, :], ps[0:PARTS * QT, place(odd), 0:P // 2].bitcast(BF16)
                                          ).then_inc(S("max_free"), 1)

                def event(number, odd, h, p, what, dh, c):
                    if what == "chunk":
                        reduce_chunk(number, odd, h + dh, (p + dh) % 2, c)
                    else:
                        keep_turned(number, odd, (p + dh) % 2)

                for e, (what, dh, c) in enumerate(at.first):
                    event(e, e, 0, 0, what, dh, c)

                def slot(h, p, has_next, has_next2):
                    if has_next:
                        for e, (what, dh, c) in enumerate(at.beside if has_next2 else at.beside_last):
                            event(at.number(h, e), at.number(p, e), h, p, what, dh, c)
                head_pairs(dve, slot)

                dve.wait_ge(S("sums_loaded"), 64)
                link(nc.vector.tensor_tensor(nd[:, 0, :, :], nd[:, 0, :, :], nd[:, 1, :, :], ALU.add))
                link(nc.vector.reciprocal(nd[:, 1, 1, :], nd[:, 0, 1, :]))
                link(nc.vector.tensor_tensor(nd[:, 1, 0, :], nd[:, 0, 0, :], nd[:, 1, 1, :], ALU.mult))
                nc.vector.tensor_scalar_add(nd[:, 0, 0, :], nd[:, 1, 0, :], v_bias).then_inc(sem("attended"), 1)
                for half in range(2):
                    dve.wait_ge(sem("product_out"), 2 * ATT.index(at.name) + 1 + half)
                    product_out(V_BANK + half, half, out_bias, gate, "tokens_done",
                                2 * ATT.index(at.name) + 1 + half)

            def bias_col(name, k):
                return cols[:, col[name] + k:col[name] + k + 1]

            pipeline("own", normalise, None, project)
            attention(attentions["own"], bias_col("L0_xcond_qkv_b", 2), "self_o", 0)
            pipeline("cross", normalise, None, project)
            attention(attentions["cross"], bias_col("L0_xcond_kv_b", 1), "cross_o", None)
            pipeline("mlp", normalise, None, project)
            pipeline("last", normalise, None, project)
            attention(attentions["last"], bias_col("L1_xcond_bkv", 1), "last", None)

        @block.tensor
        def _(pe):
            pe.wait_ge(sem("rows_loaded"), 16 * len(BIAS_ROWS))
            pe.wait_ge(sem("identities"), 2)
            nc.tensor.transpose(ps[:, 0, 0:NCOL], rows[0:NCOL, :], ident[0:NCOL, 0:NCOL]).then_inc(sem("cols_turned"), 1)
            pe.wait_ge(sem("weights_loaded"), 16 * len(w))
            pe.wait_ge(sem("silu_ready"), 1)
            for k, (name, b, s, _, _) in enumerate(MODS):
                nc.tensor.matmul(ps[:, 1, k:k + 1], w[name][:, b, :], silu[:, 3:4], start=True, stop=True)
                nc.tensor.matmul(ps[:, 1, 4 + k:5 + k], w[name][:, s, :], silu[:, 3:4], start=True, stop=True)
            for k, j in enumerate(GATES):
                last = nc.tensor.matmul(ps[:, 2, k * P:(k + 1) * P], silu_wide[:, :], w["L0_xcond_ada_w"][:, j, :],
                                        start=True, stop=True)
            last.then_inc(sem("mods_product"), 1)
            pe.wait_ge(sem("mods_ready"), 3)

            def turn(c):
                if c.eps is not None:
                    pe.wait_ge(sem("normalised"), c.norm_upto)
                else:
                    pe.wait_ge(sem(f"ctx_loaded{c.load % 2}"), ctx_ready[c.i])
                if c.i >= 2:
                    pe.wait_ge(sem("h_t_ready"), c.i - 1)
                for t, r in enumerate(c.tiles):
                    src = xh[0:r, c.i % 2, t, :] if c.eps is not None else chunk_source(c, t)
                    last = nc.tensor.transpose(ps[:, T_BANK + c.i % 2, t * P:t * P + r], src, ident[0:r, 0:r])
                last.then_inc(sem("turned"), 1)

            def project(c):
                pe.wait_ge(sem("h_t_ready"), c.i + 1)
                src = h_t[:, c.i % 2, 0:c.rows]
                if c.mlp:
                    for f in range(4):
                        k = c.pj + f
                        pe.wait_ge(sem("projected_free"), k - 1)
                        nc.tensor.matmul(ps[:, J_BANK + k % 2, :], w["L0_xcond_mlp_w1"][:, f, :], src,
                                         start=True, stop=True).then_inc(sem("projected"), 1)
                    pe.wait_ge(sem("projected_free"), c.pj + 4)
                    pe.wait_ge(sem("values_out"), c.vj - 1)
                    for t in range(4):
                        for f in range(4):
                            last = nc.tensor.matmul(ps[:, V_BANK + c.vj % 2, t * P:(t + 1) * P],
                                                    hid[:, f, t * P:(t + 1) * P], w["L0_xcond_mlp_w2"][:, f, :],
                                                    start=(f == 0), stop=(f == 3))
                    last.then_inc(sem("valued"), 1)
                    return
                for k, (weights, _, _, _) in zip(range(c.pj, c.pj_upto), c.projections):
                    if k >= 2:
                        pe.wait_ge(sem("projected_free"), k - 1)
                    last = nc.tensor.matmul(ps[:, J_BANK + k % 2, 0:c.rows], weights, src, start=True, stop=True)
                    last.then_inc(sem("projected"), 1)
                if c.values is not None:
                    if c.vj >= 2:
                        pe.wait_ge(sem("values_out"), c.vj - 1)
                    for t, r in enumerate(c.tiles):
                        last = nc.tensor.matmul(ps[0:r, V_BANK + c.vj % 2, t * P:(t + 1) * P],
                                                h_t[:, c.i % 2, t * P:t * P + r], c.values, start=True, stop=True)
                    last.then_inc(sem("valued"), 1)

            def attention(at, weights):
                S = lambda n: sem(f"{at.name}_{n}")

                def place(number):
                    return M_BANK + 2 * (number % 2)

                def max_chunk(number, odd, p, c, loaded):
                    t, c0, width = at.max_chunks[c]
                    if c == 0:
                        pe.wait_ge(S(f"for_max{p}"), 16 * PARTS * (2 if at.small else 1) * loaded)
                    if not at.small and t == 0:
                        for j, (a, b) in enumerate(at.pieces):
                            if max(c0 - 1, 0) < b * P and a * P < c0 + width and (c0 == 0 or a * P >= c0):
                                pe.wait_ge(S(f"keys{p}_{j}"), 16 * PARTS * loaded)
                    pe.wait_ge(S("max_free"), number + 1)
                    k0 = at.max_keys + c0
                    for n in range(0, width, HALF):
                        m = min(HALF, width - n)
                        last = nc.tensor.matmul(ps[:, place(odd) + n // HALF, 0:m], qm[p][0:MROW, t * P:(t + 1) * P],
                                                kh[p][0:MROW, k0 + n:k0 + n + m], start=True, stop=True)
                    last.then_inc(S("max_scored"), 1)

                def turn_max(number, odd, h):
                    pe.wait_ge(S("max_split"), h + 1)
                    pe.wait_ge(S("max_free"), number + 1)
                    nc.tensor.transpose(ps[0:PARTS * QT, place(odd), 0:P // 2].bitcast(BF16),
                                        max_parts[:, :, :].rearrange("p j t -> p (j t)"), ident16[:, :]
                                        ).then_inc(S("max_scored"), 1)

                def event(number, odd, h, p, what, dh, c, loaded):
                    if what == "chunk":
                        max_chunk(number, odd, (p + dh) % 2, c, loaded[dh])
                    else:
                        turn_max(number, odd, h + dh)

                def ready(p, loaded):
                    pe.wait_ge(S(f"queries{p}"), 16 * PARTS * loaded)
                    if at.small:
                        pe.wait_ge(S(f"keys{p}_0"), 16 * PARTS * loaded)
                    pe.wait_ge(S(f"max_loaded{p}"), 16 * PARTS * loaded)

                def score(h, p, u):
                    kt, half = u // 2, u % 2
                    pe.wait_ge(S("exps"), at.units * h + u + 1)
                    nc.tensor.matmul(ps[:, S_BANK + u % 2, :], kh[p][0:KROWS, kt * P:(kt + 1) * P],
                                     qh[p][0:KROWS, half * HALF:(half + 1) * HALF], start=True, stop=True
                                     ).then_inc(S("scored"), 1)

                def values(h, p, b):
                    if b == 0:
                        pe.wait_ge(S("values"), h + 1)
                        pe.wait_ge(S("closed"), h + 1)
                    us = at.batches[b]
                    pe.wait_ge(S("exps"), at.units * h + us[-1] + 1 + 2)
                    for n, u in enumerate(us):
                        g = u % 4
                        last = nc.tensor.matmul(ps[BLOCK * g:BLOCK * g + VW, O_BANK + p, :], vh[p][:, u // 2, :],
                                                probs[:, b % 2, n, :], start=(u < 4), stop=(u + 4 >= at.units))
                    last.then_inc(S("summed"), 1)

                for e, (what, dh, c) in enumerate(at.first):
                    event(e, e, 0, 0, what, dh, c, (1, 1))
                ready(0, 1)
                for u in at.batches[0]:
                    score(0, 0, u)

                def slot(h, p, has_next, has_next2, loaded):
                    q = 1 - p
                    events = at.beside if has_next2 else at.beside_last if has_next else []
                    for b in range(at.nb):
                        todo = [(h, p, u) for u in at.batches[b + 1]] if b + 1 < at.nb else []
                        if b + 1 == at.nb and has_next:
                            ready(q, loaded[1])
                            todo = [(h + 1, q, u) for u in at.batches[0]]
                        now = at.events_at(b, events)
                        for part in range(2):
                            for one in todo[2 * part:2 * part + 2]:
                                score(*one)
                            if part:
                                values(h, p, b)
                            for e, (what, dh, c) in (now[:2], now[2:])[part]:
                                event(at.number(h, e), at.number(p, e), h, p, what, dh, c, loaded)

                with pe.Fori(0, HEADS // 2 - 1) as i:
                    slot(2 * i, 0, True, True, (None, i + 1, i + 2))
                    slot(2 * i + 1, 1, True, True, (None, i + 2, i + 2))
                slot(HEADS - 2, 0, True, False, (None, HEADS // 2, None))
                slot(HEADS - 1, 1, False, False, None)

                pe.wait_ge(sem("attended"), ATT.index(at.name) + 1)
                for half in range(2):
                    for t in range(4):
                        q0 = (4 * half + t) * P
                        last = nc.tensor.matmul(ps[:, V_BANK + half, t * P:(t + 1) * P], nd[:, 0, 0, q0:q0 + P],
                                                weights, start=True, stop=True)
                    last.then_inc(sem("product_out"), 1)
                if at.name != ATT[-1]:
                    pe.wait_ge(sem("tokens_done"), 2 * ATT.index(at.name) + 2)

            pipeline("own", None, turn, project)
            pe.wait_ge(sem("values_out"), GROUPS["own"][-1].vj_upto)
            attention(attentions["own"], w["L0_xcond_self_o_w"][:, 0, :])
            pipeline("cross", None, turn, project)
            pe.wait_ge(sem("values_out"), GROUPS["cross"][-1].vj_upto)
            attention(attentions["cross"], w["L0_xcond_cross_o_w"][:, 0, :])
            pipeline("mlp", None, turn, project)
            pipeline("last", None, turn, project)
            pe.wait_ge(sem("values_out"), GROUPS["last"][-1].vj_upto)
            attention(attentions["last"], w["L1_xcond_Wp"][:, 0, :])


_INS = ['x', 'cond_1024', 'ctx_1024', 'L0_xcond_ada_w', 'L0_xcond_ada_b', 'L0_xcond_qkv_w', 'L0_xcond_qkv_b',
        'L0_xcond_self_o_w', 'L0_xcond_self_o_b', 'L0_xcond_norm2_g', 'L0_xcond_norm2_b', 'L0_xcond_q_w',
        'L0_xcond_q_b', 'L0_xcond_kv_w', 'L0_xcond_kv_b', 'L0_xcond_cross_o_w', 'L0_xcond_cross_o_b',
        'L0_xcond_mlp_w1', 'L0_xcond_mlp_b1', 'L0_xcond_mlp_w2', 'L0_xcond_mlp_b2', 'L1_xcond_Wq', 'L1_xcond_bq',
        'L1_xcond_Wkv', 'L1_xcond_bkv', 'L1_xcond_Wp', 'L1_xcond_bp', 'L1_xcond_Wss_q', 'L1_xcond_bss_q',
        'L1_xcond_Wss_kv', 'L1_xcond_bss_kv']
_OUT_SHAPE = (1, 1024, 128)


def kernel(**inputs):
    import numpy as _np
    import concourse.bacc as _bacc
    from concourse import mybir as _mybir
    from concourse.bass_utils import run_bass_kernel_spmd as _run

    nc = _bacc.Bacc("TRN2", target_bir_lowering=False, num_devices=1)
    arrays, aps = {}, {}
    for name in _INS:
        v = _np.ascontiguousarray(inputs[name])
        arrays[f"in_{name}"] = v
        aps[name] = nc.dram_tensor(f"in_{name}", v.shape, _mybir.dt.from_np(v.dtype), kind="ExternalInput").ap()
    out = nc.dram_tensor("out_0", _OUT_SHAPE, _mybir.dt.float32, kind="ExternalOutput").ap()
    pixart_program(nc, aps, out)
    r = _run(nc, [arrays], core_ids=[0])
    return r.results[0]["out_0"]
```
